# Optimizing a Trainium2 kernel written in Bass

```python
import numpy as np
import jax
import jax.numpy as jnp

def _softmax(x, axis=-1):
    return jax.nn.softmax(x, axis=axis)

def _gelu(x):
    return jax.nn.gelu(x, approximate=True)

def _silu(x):
    return jax.nn.silu(x)

def _sigmoid(x):
    return jax.nn.sigmoid(x)

def _layernorm(x, axis=-1, eps=1e-05):
    m = jnp.mean(x, axis=axis, keepdims=True)
    v = jnp.var(x, axis=axis, keepdims=True)
    return (x - m) / jnp.sqrt(v + eps)

def _scatter_add(tgt, idx, src, axis=0):
    return tgt.at[idx].add(src)

def _segment_sum(src, seg, n):
    return jax.ops.segment_sum(src, seg, n)
kernel_name = 'mk_adj_resnorm_d1_adj_r2_bde5b4'

def setup_inputs(seed: int=0):
    np.random.seed(seed)
    _w = jnp.asarray

    def _rec_inputs():
        import jax
        import jax.numpy as jnp
        _gk = jax.random.key(seed)
        x = 7.22e-05 + 1 * jax.random.normal(jax.random.fold_in(_gk, 1), (128, 64, 512), jnp.float32)
        _w = (1.0 + jnp.arange(64, dtype=jnp.float32)) ** (-0.5)
        _w = _w / _w.mean()
        _pij = jnp.clip(0.125 * _w[:, None] * _w[None, :], 0.0, 1.0)
        _a = jax.random.uniform(jax.random.fold_in(_gk, 2), (64, 64)) < _pij
        _a = jnp.logical_or(_a, jnp.eye(64, dtype=bool))
        _af = _a.astype(jnp.float32)
        adj = _af
        return (x, adj)
    x, adj = _rec_inputs()

    def _L0_gnn_setup():
        import jax, jax.numpy as jnp
        import numpy as np
        EPS = 1e-08

        def _row_stochastic_causal(A, causal_mask):
            A = A * causal_mask
            deg = jnp.maximum(A.sum(axis=-1, keepdims=True), EPS)
            return A / deg
        key = jax.random.key(seed)
        k = jax.random.split(key, 5)
        B, N, D = (4, 1024, 512)
        s = 1.0 / np.sqrt(D)
        h = jax.random.normal(k[0], (B, N, D), dtype=jnp.float32)
        W_lang = jax.random.normal(k[1], (D, D), dtype=jnp.float32) * s
        W_grav = jax.random.normal(k[2], (D, D), dtype=jnp.float32) * s
        W_V = jax.random.normal(k[3], (D, D), dtype=jnp.float32) * s
        W_O = jax.random.normal(k[4], (D, D), dtype=jnp.float32) * s
        causal_mask = jnp.tril(jnp.ones((N, N), dtype=jnp.float32))
        gate_logit = jnp.zeros((), jnp.float32)
        log_sigma = jnp.zeros((), jnp.float32)
        return {'h': h, 'causal_mask': causal_mask, 'W_lang': W_lang, 'W_grav': W_grav, 'W_V': W_V, 'W_O': W_O, 'gate_logit': gate_logit, 'log_sigma': log_sigma}
    _L0_gnn_all = _L0_gnn_setup()
    _L0_gnn_in = {k: v for k, v in _L0_gnn_all.items() if k in ('W_lang', 'W_grav', 'W_V', 'W_O', 'gate_logit', 'log_sigma')}
    del _L0_gnn_all
    return {'x': x, 'adj': adj, 'L0_gnn_W_lang': _L0_gnn_in['W_lang'], 'L0_gnn_W_grav': _L0_gnn_in['W_grav'], 'L0_gnn_W_V': _L0_gnn_in['W_V'], 'L0_gnn_W_O': _L0_gnn_in['W_O'], 'L0_gnn_gate_logit': _L0_gnn_in['gate_logit'], 'L0_gnn_log_sigma': _L0_gnn_in['log_sigma']}

def reference(x, adj, L0_gnn_W_lang, L0_gnn_W_grav, L0_gnn_W_V, L0_gnn_W_O, L0_gnn_gate_logit, L0_gnn_log_sigma):
    import jax
    import jax.numpy as jnp

    def _L0_gnn_ref(h, causal_mask, W_lang, W_grav, W_V, W_O, gate_logit, log_sigma):
        import jax, jax.numpy as jnp
        import numpy as np
        EPS = 1e-08

        def _row_stochastic_causal(A, causal_mask):
            A = A * causal_mask
            deg = jnp.maximum(A.sum(axis=-1, keepdims=True), EPS)
            return A / deg
        z_l = jnp.einsum('bnd,ed->bne', h, W_lang)
        z_g = jnp.einsum('bnd,ed->bne', h, W_grav)
        v = jnp.einsum('bnd,ed->bne', h, W_V)
        N = h.shape[-2]
        not_eye = 1.0 - jnp.eye(N, dtype=h.dtype)
        zn = z_l / jnp.maximum(jnp.linalg.norm(z_l, axis=-1, keepdims=True), EPS)
        A_l = jnp.maximum(jnp.einsum('bnd,bmd->bnm', zn, zn), 0.0) * not_eye
        sq = jnp.sum(z_g * z_g, axis=-1, keepdims=True)
        d2 = jnp.maximum(sq + jnp.swapaxes(sq, -1, -2) - 2.0 * jnp.einsum('bnd,bmd->bnm', z_g, z_g), 0.0)
        sigma = jnp.exp(log_sigma)
        A_g = jnp.exp(-d2 / (2.0 * sigma * sigma)) * not_eye
        K_l = _row_stochastic_causal(A_l, causal_mask)
        K_g = _row_stochastic_causal(A_g, causal_mask)
        w_l = jax.nn.sigmoid(gate_logit)
        K = w_l * K_l + (1.0 - w_l) * K_g
        out = jnp.einsum('bnm,bmd->bnd', K, v)
        return jnp.einsum('bnd,ed->bne', out, W_O)
    x = _layernorm(x + _L0_gnn_ref(x, adj, L0_gnn_W_lang, L0_gnn_W_grav, L0_gnn_W_V, L0_gnn_W_O, L0_gnn_gate_logit, L0_gnn_log_sigma), axis=-1)
    return x

_drawn_inputs = setup_inputs


def setup_inputs(seed=0):
    import zlib

    import numpy as np

    out = dict(_drawn_inputs(seed))
    spreads = {}
    factors = {}
    for name, (base, spread) in spreads.items():
        noise = np.random.default_rng([zlib.crc32(name.encode()), seed]).standard_normal(out[name].shape)
        drawn = base * np.exp(spread * noise) if base else spread * noise
        out[name] = jnp.asarray(drawn.astype(out[name].dtype))
    for name, factor in factors.items():
        out[name] = (out[name] * factor).astype(out[name].dtype)
    return out
```

```python
from contextlib import ExitStack

import concourse.bass as bass
from concourse import mybir

ALU = mybir.AluOpType
ACT = mybir.ActivationFunctionType
AX_X = mybir.AxisListType.X
F32 = mybir.dt.float32
F32R = mybir.dt.float32r

P = 128
EPS = 1e-8
LN_EPS = 1e-5
DMA = 16


def graph_attention_kernel(
    nc: bass.Bass,
    x: bass.AP,
    adj: bass.AP,
    w_lang: bass.AP,
    w_grav: bass.AP,
    w_v: bass.AP,
    w_o: bass.AP,
    gate_logit: bass.AP,
    log_sigma: bass.AP,
    out: bass.AP,
):
    B, N, D = x.shape
    C = D // P
    T = 4
    GT = T * P
    G = B * N // GT
    PAIRS = T // 2
    assert 2 * N == P and D == 512 and B * N == G * GT and G % 2 == 0

    row_start = [sum(C - r for r in range(i)) for i in range(C)]
    BLOCKS = C * (C + 1) // 2

    def block_of(i, j):
        return row_start[i] + j - i

    YU = 2 * C + T

    x_t = x.rearrange("b n d -> (b n) d").rearrange("(g t p) d -> g p t d", t=T, p=P)
    out_t = out.rearrange("b n d -> (b n) d").rearrange("(g t p) d -> g p t d", t=T, p=P)

    def weight_rows(w):
        return w.rearrange("(c p) d -> p c d", p=P)

    with ExitStack() as ctx:
        def sb(name, shape, dt=F32):
            return ctx.enter_context(nc.sbuf_tensor(name, shape, dt))

        def bank(name):
            return ctx.enter_context(nc.psum_tensor(name, [P, 512], F32))

        def sem(name):
            return ctx.enter_context(nc.semaphore(name))

        ident = sb("ident", [P, P])
        eye2 = sb("eye2", [P, N])
        half_ones = sb("half_ones", [P, P])
        mask2 = sb("mask2", [P, N])
        neg_half = sb("neg_half", [P, 2 * T])
        gates = sb("gates", [P, 8])
        w_lang_gate, w_grav_gate, neg_inv_two_var = gates[:, 3:4], gates[:, 4:5], gates[:, 7:8]

        tri_hi = sb("tri_hi", [P, 2, BLOCKS, P], F32R)
        tri_lo = sb("tri_lo", [P, 2, BLOCKS, P], F32R)
        wvo_hi = sb("wvo_hi", [P, C, D], F32R)
        wvo_lo = sb("wvo_lo", [P, C, D], F32R)

        x_in = [sb(f"x_in{i}", [P, T, D]) for i in range(2)]
        x_res = [sb(f"x_res{i}", [P, T, D]) for i in range(2)]
        xt_hi = [sb(f"xt_hi{i}", [P, C, GT], F32R) for i in range(2)]
        xt_lo = [sb(f"xt_lo{i}", [P, C, GT], F32R) for i in range(2)]
        y_hi = sb("y_hi", [P, C, 2, GT], F32R)
        y_lo = sb("y_lo", [P, C, 2, GT], F32R)
        u_hi = sb("u_hi", [P, T, D], F32R)
        u_lo = sb("u_lo", [P, T, D], F32R)

        raw = {"lang": x_res[0], "grav": x_res[1], "v": x_in[1], "o": sb("w_o_raw", [P, C, D])}
        split = {
            "lang": (y_hi[:, :, 0, :], y_lo[:, :, 0, :]),
            "grav": (y_hi[:, :, 1, :], y_lo[:, :, 1, :]),
            "v": (xt_hi[1], xt_lo[1]),
        }

        p_sb = sb("p_sb", [P, PAIRS, 2, 2, P])
        s_sb = sb("s_sb", [P, 2, T, N])
        sdiag = sb("sdiag", [P, 2, T, N])
        sq = sb("sq", [P, 2, T])
        sq_clamped = sb("sq_clamped", [P, T])
        vec = sb("vec", [P, 2, T])
        numer = sb("numer", [P, 2, T])
        dvec = sb("dvec", [P, 2, T, N])
        att = sb("att", [P, 2, T, N])
        deg = sb("deg", [P, 2, T])
        deg_clamped = sb("deg_clamped", [P, 2, T])
        deg_inv = sb("deg_inv", [P, 2, T])
        row_scale = sb("row_scale", [P, 2, T])
        k_sb = sb("k_sb", [P, T, P])
        kt_hi = sb("kt_hi", [P, T, P], F32R)
        kt_lo = sb("kt_lo", [P, T, P], F32R)
        stats = sb("stats", [P, T, 6])
        mean_var = sb("mean_var", [P, T, 2])
        var_eps = sb("var_eps", [P, T])
        rstd = sb("rstd", [P, T])
        shift = sb("shift", [P, T])

        RING = 3
        yu_bank = [bank(f"yu_bank{i}") for i in range(RING)]
        assert YU % RING == 0
        xt_bank = bank("xt_bank")
        p_bank = bank("p_bank")
        pt_bank = bank("pt_bank")
        rk_bank = bank("rk_bank")
        o_bank = bank("o_bank")

        w_loaded = {k: sem(f"w_{k}_loaded") for k in ("lang", "grav", "v", "o")}
        w_hi = {k: sem(f"w_{k}_hi") for k in split}
        w_lo = {k: sem(f"w_{k}_lo") for k in split}
        small_loaded = sem("small_loaded")
        ident_ready = sem("ident_ready")
        consts_ready = sem("consts_ready")
        pool_step = sem("pool_step")
        exps_ready = sem("exps_ready")
        gates_step = sem("gates_step")
        gates_ready = sem("gates_ready")
        x_in_loaded = [sem(f"x_in_loaded{i}") for i in range(2)]
        x_res_loaded = [sem(f"x_res_loaded{i}") for i in range(2)]
        stored = sem("stored")
        xt_ready, xt_hi_done, xt_lo_done = sem("xt_ready"), sem("xt_hi_done"), sem("xt_lo_done")
        yu_ready, yu_hi_done, yu_lo_done = sem("yu_ready"), sem("yu_hi_done"), sem("yu_lo_done")
        p_ready, p_saved = sem("p_ready"), sem("p_saved")
        pt_ready, s_ready = sem("pt_ready"), sem("s_ready")
        norms_step = sem("norms_step")
        sq_ready = sem("sq_ready")
        vec_ready = sem("vec_ready")
        row_scale_ready = sem("row_scale_ready")
        inv_norm_ready = sem("inv_norm_ready")
        dvec_ready = sem("dvec_ready")
        rows_ready = sem("rows_ready")
        att_step = sem("att_step")
        dist_ready = sem("dist_ready")
        exp_done = sem("exp_done")
        k_ready = sem("k_ready")
        kt_ready, kt_hi_done, kt_lo_done = sem("kt_ready"), sem("kt_hi_done"), sem("kt_lo_done")
        o_ready, o_added = sem("o_ready"), sem("o_added")
        stats_ready, moments_ready = sem("stats_ready"), sem("moments_ready")
        var_ready = sem("var_ready")
        rstd_ready = sem("rstd_ready")
        shift_ready = sem("shift_ready")
        normed = sem("normed")

        def yu_before(i):
            return YU * (i + 1)

        def xt_before(g):
            return C * (g + 1)

        def loads_of(g, parity):
            return DMA // 2 * (g - parity) + DMA

        def each_iteration(eng, body):
            body(0, 0, first=True)
            with eng.Fori(1, G - 2, 2) as i:
                body(i, 1)
                body(i + 1, 0)
            body(G - 1, 1, last=True)
            body(G, 0, tail=True)

        block = ctx.enter_context(nc.Block())

        @block.sync
        def _(sp):
            for k, w in (("lang", w_lang), ("grav", w_grav), ("o", w_o), ("v", w_v)):
                sp.dma_start(raw[k][:], weight_rows(w)).then_inc(w_loaded[k], DMA)
            sp.dma_start(x_in[0][:], x_t[0]).then_inc(x_in_loaded[0], DMA)
            for h in range(2):
                sp.dma_start(mask2[h * N:(h + 1) * N, :], adj).then_inc(small_loaded, DMA)
            with nc.allow_non_contiguous_dma(reason="two scalars"):
                sp.dma_start(gates[:, 0:1], gate_logit.to_broadcast([P, 1])).then_inc(small_loaded, DMA)
                sp.dma_start(gates[:, 1:2], log_sigma.to_broadcast([P, 1])).then_inc(small_loaded, DMA)
            sp.wait_ge(w_hi["lang"], C)
            sp.wait_ge(w_lo["lang"], C)
            sp.dma_start(x_res[0][:], x_t[0]).then_inc(x_res_loaded[0], DMA)

            def body(i, parity, first=False, last=False, tail=False):
                if first:
                    for k in ("v", "grav"):
                        sp.wait_ge(w_hi[k], C)
                        sp.wait_ge(w_lo[k], C)
                if not last and not tail:
                    if not first:
                        sp.wait_ge(xt_ready, xt_before(i))
                    sp.dma_start(x_in[1 - parity][:], x_t[i + 1]).then_inc(x_in_loaded[1 - parity], DMA)
                if not first:
                    for t in range(T):
                        sp.wait_ge(normed, T * (i - 1) + t + 1)
                        sp.dma_start(out_t[i - 1, :, t, :], x_res[1 - parity][:, t, :]).then_inc(stored, DMA)
                    sp.wait_ge(stored, DMA * T * i)
                if not last and not tail:
                    sp.dma_start(x_res[1 - parity][:], x_t[i + 1]).then_inc(x_res_loaded[1 - parity], DMA)

            each_iteration(sp, body)

        @block.gpsimd
        def _(pool):
            n = [0]

            def ordered(ins):
                n[0] += 1
                ins.then_inc(pool_step, 1)
                pool.wait_ge(pool_step, n[0])

            ordered(nc.gpsimd.memset(ident[:], 0.0))
            ordered(nc.gpsimd.affine_select(out=ident[:], in_=ident[:], compare_op=ALU.not_equal, fill=1.0,
                                            base=0, pattern=[[-1, P]], channel_multiplier=1))
            nc.gpsimd.engine_nop().then_inc(ident_ready, 1)
            ordered(nc.gpsimd.memset(half_ones[:], 0.0))
            ordered(nc.gpsimd.memset(half_ones[0:N, 0:N], 1.0))
            ordered(nc.gpsimd.memset(half_ones[N:P, N:P], 1.0))
            ordered(nc.gpsimd.memset(k_sb[:], 0.0))
            ordered(nc.gpsimd.memset(neg_half[:], -0.5))
            ordered(nc.gpsimd.memset(numer[:], 0.0))
            ordered(nc.gpsimd.memset(eye2[:], 0.0))
            pool.wait_ge(small_loaded, 4 * DMA)
            for h in range(2):
                for buf, fill in ((eye2, 1.0), (mask2, 0.0)):
                    ordered(nc.gpsimd.affine_select(
                        out=buf[:], in_=buf[:], compare_op=ALU.not_equal, fill=fill, base=-N * h,
                        pattern=[[-1, N]], channel_multiplier=1))
            nc.gpsimd.engine_nop().then_inc(consts_ready, 1)

            def body(i, parity, first=False, last=False, tail=False):
                if not first:
                    pool.wait_ge(var_ready, i)
                    nc.gpsimd.tensor_tensor(rstd[:], var_eps[:], neg_half[:, 0:T],
                                            ALU.pow).then_inc(rstd_ready, 1)
                if not tail:
                    pool.wait_ge(sq_ready, i + 1)
                    nc.gpsimd.tensor_tensor(vec[:, 0, :], sq_clamped[:], neg_half[:, 0:T],
                                            ALU.pow).then_inc(inv_norm_ready, 1)

            each_iteration(pool, body)

        @block.scalar
        def _(act):
            act.wait_ge(small_loaded, 4 * DMA)
            nc.scalar.activation(gates[:, 2:3], gates[:, 0:1], ACT.Exp, scale=-1.0).then_inc(exps_ready, 1)
            nc.scalar.activation(gates[:, 5:6], gates[:, 1:2], ACT.Exp).then_inc(exps_ready, 1)

            def weight_hi(k):
                act.wait_ge(w_loaded[k], DMA)
                for c in range(C):
                    nc.scalar.copy(split[k][0][:, c, :], raw[k][:, c, :]).then_inc(w_hi[k], 1)

            def hi_of_bank(dst, src, ready, n, done):
                act.wait_ge(ready, n)
                nc.scalar.copy(dst, src).then_inc(done, 1)

            weight_hi("lang")
            weight_hi("grav")
            weight_hi("v")
            for c in range(C):
                hi_of_bank(u_hi[:, c, :], xt_bank[:], xt_ready, c + 1, xt_hi_done)
            for k in range(2):
                for r in range(C):
                    n, b = k * C + r, yu_bank[(k * C + r) % RING]
                    act.wait_ge(yu_ready, n + 1)
                    done = nc.scalar.mul(tri_hi[:, k, row_start[r], :], b[:, 0:P], 0.5)
                    if r < C - 1:
                        done = nc.scalar.copy(
                            tri_hi[:, k, row_start[r] + 1:row_start[r] + C - r, :].rearrange("p b d -> p (b d)"),
                            b[:, P:(C - r) * P])
                    done.then_inc(yu_hi_done, 1)
            for c in range(C):
                hi_of_bank(wvo_hi[:, c, :], yu_bank[(2 * C + c) % RING][:], yu_ready, 2 * C + c + 1, yu_hi_done)
            for c in range(C):
                hi_of_bank(xt_hi[0][:, c, :], xt_bank[:], xt_ready, xt_before(0) + c + 1, xt_hi_done)

            def body(i, parity, first=False, last=False, tail=False):
                main, finish, ahead = not tail, not first, not last and not tail

                def y_hi_of(n):
                    if main:
                        k, j = divmod(n, C)
                        hi_of_bank(y_hi[:, j, k, :], yu_bank[n % RING][:], yu_ready, yu_before(i) + n + 1, yu_hi_done)

                def u_hi_of(t):
                    if main:
                        n = 2 * C + t
                        hi_of_bank(u_hi[:, t, :], yu_bank[n % RING][:], yu_ready, yu_before(i) + n + 1, yu_hi_done)

                def xt_hi_of(c):
                    if ahead:
                        hi_of_bank(xt_hi[1 - parity][:, c, :], xt_bank[:], xt_ready, xt_before(i + 1) + c + 1, xt_hi_done)

                def save_p(pair):
                    if main:
                        act.wait_ge(p_ready, PAIRS * i + pair + 1)
                        if not first:
                            act.wait_ge(s_ready, PAIRS * (i - 1) + pair + 1)
                        nc.scalar.copy(p_sb[:, pair].rearrange("p a k m -> p (a k m)"),
                                       p_bank[:]).then_inc(p_saved, 1)

                for n in range(C):
                    y_hi_of(n)
                if finish:
                    act.wait_ge(dist_ready, i)
                    nc.scalar.activation(att[:, 1], att[:, 1], ACT.Exp, scale=neg_inv_two_var).then_inc(exp_done, 1)
                y_hi_of(C)
                xt_hi_of(0)
                y_hi_of(C + 1)
                xt_hi_of(1)
                y_hi_of(C + 2)
                if finish:
                    hi_of_bank(kt_hi[:].rearrange("p t n -> p (t n)"), rk_bank[:], kt_ready, i, kt_hi_done)
                xt_hi_of(2)
                y_hi_of(C + 3)
                xt_hi_of(3)
                u_hi_of(0)
                save_p(0)
                u_hi_of(1)
                save_p(1)
                u_hi_of(2)
                u_hi_of(3)
                if finish:
                    act.wait_ge(shift_ready, i)
                    for t in range(T):
                        nc.scalar.activation(
                            x_res[1 - parity][:, t, :], x_res[1 - parity][:, t, :], ACT.Identity,
                            scale=rstd[:, t:t + 1], bias=shift[:, t:t + 1]).then_inc(normed, 1)

            each_iteration(act, body)

        @block.vector
        def _(dve):
            def lo_of_bank(dst, src, hi, hi_done, n, done):
                dve.wait_ge(hi_done, n)
                nc.vector.tensor_sub(dst, src, hi).then_inc(done, 1)

            def weight_lo(k):
                for c in range(C):
                    lo_of_bank(split[k][1][:, c, :], raw[k][:, c, :], split[k][0][:, c, :], w_hi[k], c + 1, w_lo[k])

            dve.wait_ge(exps_ready, 2)
            nc.vector.tensor_scalar_add(gates[:, 3:4], gates[:, 2:3], 1.0)
            nc.vector.tensor_scalar(gates[:, 6:7], gates[:, 5:6], gates[:, 5:6], 2.0, ALU.mult,
                                    ALU.mult).then_inc(gates_step, 1)
            dve.wait_ge(gates_step, 1)
            nc.vector.reciprocal(gates[:, 3:4], gates[:, 3:4])
            nc.vector.reciprocal(gates[:, 7:8], gates[:, 6:7]).then_inc(gates_step, 1)
            dve.wait_ge(gates_step, 2)
            nc.vector.tensor_scalar(gates[:, 4:5], gates[:, 3:4], -1.0, 1.0, ALU.mult, ALU.add)
            nc.vector.tensor_scalar_mul(gates[:, 7:8], gates[:, 7:8], -1.0).then_inc(gates_step, 1)
            dve.wait_ge(gates_step, 3)
            dve.wait_ge(consts_ready, 1)
            nc.vector.tensor_scalar(numer[:, 1, :], numer[:, 1, :], w_grav_gate, None,
                                    ALU.add).then_inc(gates_ready, 1)

            weight_lo("lang")
            weight_lo("grav")
            weight_lo("v")
            for c in range(C):
                lo_of_bank(u_lo[:, c, :], xt_bank[:], u_hi[:, c, :], xt_hi_done, c + 1, xt_lo_done)
            for k in range(2):
                for r in range(C):
                    n, b = k * C + r, yu_bank[(k * C + r) % RING]
                    dve.wait_ge(yu_hi_done, n + 1)
                    done = nc.vector.scalar_tensor_tensor(
                        tri_lo[:, k, row_start[r], :], b[:, 0:P], 0.5, tri_hi[:, k, row_start[r], :],
                        ALU.mult, ALU.subtract)
                    if r < C - 1:
                        rest = slice(row_start[r] + 1, row_start[r] + C - r)
                        done = nc.vector.tensor_sub(
                            tri_lo[:, k, rest, :].rearrange("p b d -> p (b d)"), b[:, P:(C - r) * P],
                            tri_hi[:, k, rest, :].rearrange("p b d -> p (b d)"))
                    done.then_inc(yu_lo_done, 1)
            for c in range(C):
                lo_of_bank(wvo_lo[:, c, :], yu_bank[(2 * C + c) % RING][:], wvo_hi[:, c, :], yu_hi_done,
                           2 * C + c + 1, yu_lo_done)
            for c in range(C):
                lo_of_bank(xt_lo[0][:, c, :], xt_bank[:], xt_hi[0][:, c, :], xt_hi_done,
                           xt_before(0) + c + 1, xt_lo_done)

            NORMS, ATT = 2, 9

            def body(i, parity, first=False, last=False, tail=False):
                main, finish, ahead = not tail, not first, not last and not tail

                def stage(step, per_group, group):
                    n = [0]

                    def after(ins):
                        n[0] += 1
                        assert n[0] <= per_group
                        ins.then_inc(step, 1)
                        dve.wait_ge(step, per_group * group + n[0])
                    return after

                def y_lo_of(n):
                    if main:
                        k, j = divmod(n, C)
                        lo_of_bank(y_lo[:, j, k, :], yu_bank[n % RING][:], y_hi[:, j, k, :], yu_hi_done,
                                   yu_before(i) + n + 1, yu_lo_done)

                def u_lo_of(t):
                    if main:
                        n = 2 * C + t
                        lo_of_bank(u_lo[:, t, :], yu_bank[n % RING][:], u_hi[:, t, :], yu_hi_done,
                                   yu_before(i) + n + 1, yu_lo_done)

                def xt_lo_of(c):
                    if ahead:
                        lo_of_bank(xt_lo[1 - parity][:, c, :], xt_bank[:], xt_hi[1 - parity][:, c, :], xt_hi_done,
                                   xt_before(i + 1) + c + 1, xt_lo_done)

                def add_transposed(pair):
                    if main:
                        dve.wait_ge(pt_ready, PAIRS * i + pair + 1)
                        for h in range(2):
                            rows, cols = slice(h * N, (h + 1) * N), slice(h * N, (h + 1) * N)
                            for a in range(2):
                                done = nc.vector.tensor_add(
                                    s_sb[rows, :, 2 * pair + a, :],
                                    pt_bank[rows, 2 * a * P:2 * (a + 1) * P].rearrange("p (k m) -> p k m", k=2)[:, :, cols],
                                    p_sb[rows, pair, a, :, cols])
                        done.then_inc(s_ready, 1)

                def norms():
                    if main:
                        after = stage(norms_step, NORMS, i)
                        dve.wait_ge(s_ready, PAIRS * (i + 1))
                        after(nc.vector.tensor_mul(
                            sdiag[:].rearrange("p k t m -> p (k t) m"), s_sb[:].rearrange("p k t m -> p (k t) m"),
                            eye2[:].unsqueeze(1).to_broadcast([P, 2 * T, N])))
                        after(nc.vector.reduce_sum(sq[:].rearrange("p k t -> p (k t)"),
                                                   sdiag[:].rearrange("p k t m -> p (k t) m"), AX_X))
                        nc.vector.tensor_scalar_max(sq_clamped[:], sq[:, 0, :], EPS * EPS).then_inc(sq_ready, 1)

                def spread_norms():
                    if finish:
                        nc.vector.tensor_copy(vec[:, 1, :], sq[:, 1, :]).then_inc(vec_ready, 1)
                        dve.wait_ge(vec_ready, i)
                        dve.wait_ge(inv_norm_ready, i)
                        nc.vector.tensor_scalar(numer[:, 0, :], vec[:, 0, :], w_lang_gate, None, ALU.mult)
                        nc.vector.tensor_mul(
                            dvec[:].rearrange("p k t m -> p (k t) m"),
                            eye2[:].unsqueeze(1).to_broadcast([P, 2 * T, N]),
                            vec[:].rearrange("p k t -> p (k t)").unsqueeze(2).to_broadcast([P, 2 * T, N]),
                        ).then_inc(dvec_ready, 1)

                after_att = stage(att_step, ATT, i - 1) if finish else None

                def distances():
                    if finish:
                        dve.wait_ge(rows_ready, i)
                        rows = rk_bank[:].rearrange("p (k t m) -> p k t m", k=2, t=T)
                        after_att(nc.vector.scalar_tensor_tensor(
                            att[:, 1], s_sb[:, 1], -2.0, rows[:, 1], ALU.mult, ALU.add))
                        after_att(nc.vector.tensor_add(
                            att[:, 1], att[:, 1], vec[:, 1, :].unsqueeze(2).to_broadcast([P, T, N])))
                        nc.vector.tensor_scalar_max(att[:, 1], att[:, 1], 0.0).then_inc(dist_ready, 1)
                        after_att(nc.vector.scalar_tensor_tensor(
                            att[:, 0], s_sb[:, 0], 0.0, rows[:, 0], ALU.max, ALU.mult))

                def mix_kernels():
                    if finish:
                        dve.wait_ge(exp_done, i)
                        flat = att[:].rearrange("p k t m -> p (k t) m")
                        after_att(nc.vector.tensor_mul(flat, flat, mask2[:].unsqueeze(1).to_broadcast([P, 2 * T, N])))
                        after_att(nc.vector.reduce_sum(deg[:].rearrange("p k t -> p (k t)"), flat, AX_X))
                        after_att(nc.vector.tensor_mul(deg[:, 0, :], deg[:, 0, :], vec[:, 0, :]))
                        after_att(nc.vector.tensor_scalar_max(deg_clamped[:], deg[:], EPS))
                        after_att(nc.vector.reciprocal(deg_inv[:], deg_clamped[:]))
                        nc.vector.tensor_mul(row_scale[:], deg_inv[:], numer[:]).then_inc(row_scale_ready, 1)
                        dve.wait_ge(row_scale_ready, i)
                        after_att(nc.vector.tensor_mul(
                            flat, flat, row_scale[:].rearrange("p k t -> p (k t)").unsqueeze(2).to_broadcast([P, 2 * T, N])))
                        for h in range(2):
                            rows = slice(h * N, (h + 1) * N)
                            done = nc.vector.tensor_add(k_sb[rows, :, h * N:(h + 1) * N], att[rows, 0], att[rows, 1])
                        done.then_inc(k_ready, 1)

                def add_residual(t):
                    if finish:
                        if t == 0:
                            dve.wait_ge(x_res_loaded[1 - parity], loads_of(i - 1, 1 - parity))
                        dve.wait_ge(o_ready, T * (i - 1) + t + 1)
                        r = x_res[1 - parity][:, t, :]
                        nc.vector.tensor_add(r, o_bank[:], r).then_inc(o_added, 1)

                def layer_stats(t):
                    if finish:
                        dve.wait_ge(o_added, T * (i - 1) + t + 1)
                        nc.vector.bn_stats(stats[:, t, :], x_res[1 - parity][:, t, :]).then_inc(stats_ready, 1)

                def wait_for_stats():
                    if finish:
                        dve.wait_ge(stats_ready, T * i)

                def layer_moments():
                    if finish:
                        for t in range(T):
                            nc.vector.bn_aggr(mean_var[:, t, :], stats[:, t, :]).then_inc(moments_ready, 1)
                        dve.wait_ge(moments_ready, T * i)
                        nc.vector.tensor_scalar_add(var_eps[:], mean_var[:, :, 1], LN_EPS).then_inc(var_ready, 1)

                def layer_shift():
                    if finish:
                        dve.wait_ge(rstd_ready, i)
                        nc.vector.scalar_tensor_tensor(shift[:], mean_var[:, :, 0], -1.0, rstd[:],
                                                       ALU.mult, ALU.mult).then_inc(shift_ready, 1)

                y_lo_of(0)
                spread_norms()
                y_lo_of(1)
                y_lo_of(2)
                distances()
                y_lo_of(3)
                y_lo_of(C)
                mix_kernels()
                xt_lo_of(0)
                y_lo_of(C + 1)
                xt_lo_of(1)
                y_lo_of(C + 2)
                if finish:
                    lo_of_bank(kt_lo[:].rearrange("p t n -> p (t n)"), rk_bank[:],
                               kt_hi[:].rearrange("p t n -> p (t n)"), kt_hi_done, i, kt_lo_done)
                xt_lo_of(2)
                y_lo_of(C + 3)
                xt_lo_of(3)
                add_residual(0)
                u_lo_of(0)
                add_residual(1)
                layer_stats(0)
                add_residual(2)
                layer_stats(1)
                u_lo_of(1)
                add_transposed(0)
                layer_stats(2)
                add_residual(3)
                layer_stats(3)
                wait_for_stats()
                u_lo_of(2)
                layer_moments()
                add_transposed(1)
                layer_shift()
                norms()
                u_lo_of(3)

            each_iteration(dve, body)

        @block.tensor
        def _(pe):
            def transpose_chunk(src, c):
                for t in range(T):
                    last = nc.tensor.transpose(xt_bank[:, t * P:(t + 1) * P], src[:, t, c * P:(c + 1) * P], ident[:])
                last.then_inc(xt_ready, 1)

            def product(dst, terms):
                for n, (lhs_t, rhs) in enumerate(terms):
                    last = nc.tensor.matmul(dst, lhs_t, rhs, start=n == 0, stop=n == len(terms) - 1)
                return last

            def three(a_hi, a_lo, b_hi, b_lo):
                return [(a_hi, b_hi), (a_hi, b_lo), (a_lo, b_hi)]

            pe.wait_ge(ident_ready, 1)
            pe.wait_ge(w_loaded["o"], DMA)
            for c in range(C):
                if c:
                    pe.wait_ge(xt_lo_done, c)
                transpose_chunk(raw["o"], c)
            for k, name in enumerate(("lang", "grav")):
                hi, lo = split[name]
                pe.wait_ge(w_lo[name], C)
                for r in range(C):
                    n = k * C + r
                    if n >= RING:
                        pe.wait_ge(yu_lo_done, n - RING + 1)
                    rows, cols = slice(r * P, (r + 1) * P), slice(r * P, D)
                    terms = []
                    for c in range(C):
                        terms += three(hi[:, c, rows], lo[:, c, rows], hi[:, c, cols], lo[:, c, cols])
                    product(yu_bank[n % RING][:, 0:D - r * P], terms).then_inc(yu_ready, 1)
            pe.wait_ge(w_lo["v"], C)
            pe.wait_ge(xt_lo_done, C)
            for r in range(C):
                n = 2 * C + r
                pe.wait_ge(yu_lo_done, n - RING + 1)
                rows = slice(r * P, (r + 1) * P)
                terms = []
                for c in range(C):
                    terms += three(split["v"][0][:, c, rows], split["v"][1][:, c, rows], u_hi[:, c, :], u_lo[:, c, :])
                product(yu_bank[n % RING][:], terms).then_inc(yu_ready, 1)
            pe.wait_ge(x_in_loaded[0], DMA)
            for c in range(C):
                if c:
                    pe.wait_ge(xt_lo_done, xt_before(0) + c)
                transpose_chunk(x_in[0], c)

            def body(i, parity, first=False, last=False, tail=False):
                main, finish, ahead = not tail, not first, not last and not tail
                hi, lo = xt_hi[parity], xt_lo[parity]

                def project(n):
                    if main:
                        k, j = divmod(n, C)
                        pe.wait_ge(yu_lo_done, yu_before(i) + n - RING + 1)
                        if k == 0:
                            pe.wait_ge(xt_lo_done, xt_before(i) + j + 1)
                        terms = []
                        for r in range(j + 1):
                            b = block_of(r, j)
                            terms += three(tri_hi[:, k, b, :], tri_lo[:, k, b, :], hi[:, r, :], lo[:, r, :])
                        product(yu_bank[n % RING][:], terms).then_inc(yu_ready, 1)

                def values(t):
                    if main:
                        n = 2 * C + t
                        pe.wait_ge(yu_lo_done, yu_before(i) + n - RING + 1)
                        tok = slice(t * P, (t + 1) * P)
                        terms = []
                        for c in range(C):
                            terms += three(hi[:, c, tok], lo[:, c, tok], wvo_hi[:, c, :], wvo_lo[:, c, :])
                        product(yu_bank[n % RING][:], terms).then_inc(yu_ready, 1)

                def transpose_ahead(c):
                    if ahead:
                        if c == 0:
                            pe.wait_ge(x_in_loaded[1 - parity], loads_of(i + 1, 1 - parity))
                        pe.wait_ge(xt_lo_done, xt_before(i + 1) + c)
                        transpose_chunk(x_in[1 - parity], c)

                def inner_products(pair):
                    if main:
                        if pair == 0:
                            pe.wait_ge(yu_lo_done, yu_before(i) + 2 * C)
                        for a in range(2):
                            tok = slice((2 * pair + a) * P, (2 * pair + a + 1) * P)
                            terms = []
                            for c in range(C):
                                terms += three(hi[:, c, tok], lo[:, c, tok], y_hi[:, c, :, tok], y_lo[:, c, :, tok])
                            done = product(p_bank[:, 2 * a * P:2 * (a + 1) * P].rearrange("p (k m) -> p k m", k=2), terms)
                        done.then_inc(p_ready, 1)

                def transpose_p(pair):
                    if main:
                        pe.wait_ge(p_saved, PAIRS * i + pair + 1)
                        if not first or pair:
                            pe.wait_ge(s_ready, PAIRS * i + pair)
                        for a in range(2):
                            for k in range(2):
                                b = 2 * a + k
                                done = nc.tensor.transpose(pt_bank[:, b * P:(b + 1) * P], p_sb[:, pair, a, k, :], ident[:])
                        done.then_inc(pt_ready, 1)

                def norms_along_rows():
                    if finish:
                        pe.wait_ge(dvec_ready, i)
                        nc.tensor.matmul(rk_bank[:], half_ones[:], dvec[:].rearrange("p k t m -> p (k t m)"),
                                         start=True, stop=True).then_inc(rows_ready, 1)

                def transpose_k():
                    if finish:
                        pe.wait_ge(k_ready, i)
                        for t in range(T):
                            done = nc.tensor.transpose(rk_bank[:, t * P:(t + 1) * P], k_sb[:, t, :], ident[:])
                        done.then_inc(kt_ready, 1)

                def attend(t):
                    if finish:
                        if t == 0:
                            pe.wait_ge(kt_lo_done, i)
                        else:
                            pe.wait_ge(o_added, T * (i - 1) + t)
                        product(o_bank[:], three(kt_hi[:, t, :], kt_lo[:, t, :], u_hi[:, t, :],
                                                 u_lo[:, t, :])).then_inc(o_ready, 1)

                project(0)
                project(1)
                project(2)
                norms_along_rows()
                project(3)
                project(C)
                transpose_ahead(0)
                project(C + 1)
                transpose_ahead(1)
                project(C + 2)
                transpose_k()
                transpose_ahead(2)
                project(C + 3)
                transpose_ahead(3)
                attend(0)
                values(0)
                attend(1)
                inner_products(0)
                attend(2)
                values(1)
                transpose_p(0)
                attend(3)
                inner_products(1)
                values(2)
                transpose_p(1)
                values(3)

            each_iteration(pe, body)


_INS = ["x", "adj", "L0_gnn_W_lang", "L0_gnn_W_grav", "L0_gnn_W_V", "L0_gnn_W_O", "L0_gnn_gate_logit",
        "L0_gnn_log_sigma"]
_OUTS = [((128, 64, 512), "float32")]


def kernel(**inputs):
    import numpy as _np
    import concourse.bacc as _bacc
    from concourse import mybir as _mybir
    from concourse.bass_utils import run_bass_kernel_spmd as _run

    nc = _bacc.Bacc("TRN2", target_bir_lowering=False, num_devices=1)
    arrays, args = {}, []
    for name in _INS:
        a = _np.ascontiguousarray(inputs[name])
        if a.ndim < 2:
            a = a.reshape(1, 1)
        arrays[f"in_{name}_dram"] = a
        args.append(nc.dram_tensor(f"in_{name}_dram", a.shape, _mybir.dt.from_np(a.dtype), kind="ExternalInput").ap())
    for i, (shape, dtype) in enumerate(_OUTS):
        dt = _mybir.dt.from_np(_np.dtype(dtype))
        args.append(nc.dram_tensor(f"out_{i}_dram", shape, dt, kind="ExternalOutput").ap())
    graph_attention_kernel(nc, *args)
    r = _run(nc, [arrays], core_ids=[0])
    got = tuple(r.results[0][f"out_{i}_dram"] for i in range(len(_OUTS)))
    return got[0]
```

```python
from contextlib import ExitStack

import concourse.bass as bass
from concourse import mybir

ALU = mybir.AluOpType
ACT = mybir.ActivationFunctionType
AX_X = mybir.AxisListType.X
F32 = mybir.dt.float32
F32R = mybir.dt.float32r

P = 128
EPS = 1e-8
LN_EPS = 1e-5
DMA = 16


def graph_attention_kernel(
    nc: bass.Bass,
    x: bass.AP,
    adj: bass.AP,
    w_lang: bass.AP,
    w_grav: bass.AP,
    w_v: bass.AP,
    w_o: bass.AP,
    gate_logit: bass.AP,
    log_sigma: bass.AP,
    out: bass.AP,
):
    B, N, D = x.shape
    C = D // P
    T = 4
    GT = T * P
    G = B * N // GT
    PAIRS = T // 2
    assert 2 * N == P and D == 512 and B * N == G * GT and G % 2 == 0

    row_start = [sum(C - r for r in range(i)) for i in range(C)]
    BLOCKS = C * (C + 1) // 2

    def block_of(i, j):
        return row_start[i] + j - i

    LANG, GRAV = 0, 1
    USES = [("y", LANG, 3), ("y", LANG, 2), ("y", GRAV, 3), ("x", 0), ("y", GRAV, 2), ("x", 1),
            ("y", LANG, 1), ("x", 2), ("y", GRAV, 1), ("x", 3), ("y", LANG, 0), ("y", GRAV, 0),
            ("u", 0), ("u", 1), ("u", 2), ("u", 3)]
    LAST_USES = [use for use in USES if use[0] != "x"]
    RING = 4
    BEFORE = C + 2 * C + C + C
    assert len(USES) % RING == 0 and BEFORE % RING == 0

    x_t = x.rearrange("b n d -> (b n) d").rearrange("(g t p) d -> g p t d", t=T, p=P)
    out_t = out.rearrange("b n d -> (b n) d").rearrange("(g t p) d -> g p t d", t=T, p=P)

    def weight_rows(w):
        return w.rearrange("(c p) d -> p c d", p=P)

    with ExitStack() as ctx:
        def sb(name, shape, dt=F32):
            return ctx.enter_context(nc.sbuf_tensor(name, shape, dt))

        def bank(name):
            return ctx.enter_context(nc.psum_tensor(name, [P, 512], F32))

        def sem(name):
            return ctx.enter_context(nc.semaphore(name))

        ident = sb("ident", [P, P])
        eye2 = sb("eye2", [P, N])
        half_ones = sb("half_ones", [P, P])
        mask2 = sb("mask2", [P, N])
        neg_half = sb("neg_half", [P, 2 * T])
        gates = sb("gates", [P, 8])
        w_lang_gate, w_grav_gate, neg_inv_two_var = gates[:, 3:4], gates[:, 4:5], gates[:, 7:8]

        tri_hi = sb("tri_hi", [P, 2, BLOCKS, P], F32R)
        tri_lo = sb("tri_lo", [P, 2, BLOCKS, P], F32R)
        wvo_hi = sb("wvo_hi", [P, C, D], F32R)
        wvo_lo = sb("wvo_lo", [P, C, D], F32R)

        x_in = [sb(f"x_in{i}", [P, T, D]) for i in range(2)]
        x_res = [sb(f"x_res{i}", [P, T, D]) for i in range(2)]
        xt_hi = [sb(f"xt_hi{i}", [P, C, GT], F32R) for i in range(2)]
        xt_lo = [sb(f"xt_lo{i}", [P, C, GT], F32R) for i in range(2)]
        y_hi = sb("y_hi", [P, C, 2, GT], F32R)
        y_lo = sb("y_lo", [P, C, 2, GT], F32R)
        u_hi = [sb(f"u_hi{i}", [P, T, D], F32R) for i in range(2)]
        u_lo = [sb(f"u_lo{i}", [P, T, D], F32R) for i in range(2)]

        raw = {"lang": x_res[0], "grav": x_res[1], "v": x_in[1], "o": sb("w_o_raw", [P, C, D])}
        split = {
            "lang": (y_hi[:, :, 0, :], y_lo[:, :, 0, :]),
            "grav": (y_hi[:, :, 1, :], y_lo[:, :, 1, :]),
            "v": (xt_hi[1], xt_lo[1]),
        }
        wo_t_hi, wo_t_lo = u_hi[0], u_lo[0]

        p_sb = sb("p_sb", [P, PAIRS, 2, 2, P])
        s_sb = sb("s_sb", [P, 2, T, N])
        sdiag = sb("sdiag", [P, 2, T, N])
        sq = sb("sq", [P, 2, T])
        sq_clamped = sb("sq_clamped", [P, T])
        vec = sb("vec", [P, 2, T])
        numer = sb("numer", [P, 2, T])
        dvec = sb("dvec", [P, 2, T, N])
        att = sb("att", [P, 2, T, N])
        deg = sb("deg", [P, 2, T])
        deg_clamped = sb("deg_clamped", [P, 2, T])
        deg_inv = sb("deg_inv", [P, 2, T])
        row_scale = sb("row_scale", [P, 2, T])
        k_sb = sb("k_sb", [P, T, P])
        kt_hi = sb("kt_hi", [P, T, P], F32R)
        kt_lo = sb("kt_lo", [P, T, P], F32R)
        stats = sb("stats", [P, T, 6])
        mean_var = sb("mean_var", [P, T, 2])
        var_eps = sb("var_eps", [P, T])
        rstd = sb("rstd", [P, T])
        shift = sb("shift", [P, T])

        ring = [bank(f"ring{i}") for i in range(RING)]
        p_bank = bank("p_bank")
        pt_bank = bank("pt_bank")
        rk_bank = bank("rk_bank")
        o_bank = bank("o_bank")

        w_loaded = {k: [sem(f"w_{k}_loaded{c}") for c in range(C)] for k in ("lang", "grav", "v", "o")}
        w_hi = {k: sem(f"w_{k}_hi") for k in split}
        w_lo = {k: sem(f"w_{k}_lo") for k in split}
        small_loaded = sem("small_loaded")
        ident_ready = sem("ident_ready")
        consts_ready = sem("consts_ready")
        pool_step = sem("pool_step")
        exps_ready = sem("exps_ready")
        gates_step = sem("gates_step")
        gates_ready = sem("gates_ready")
        x_in_loaded = [sem(f"x_in_loaded{i}") for i in range(2)]
        x_res_loaded = [sem(f"x_res_loaded{i}") for i in range(2)]
        stored = sem("stored")
        ring_ready, ring_hi, ring_lo = sem("ring_ready"), sem("ring_hi"), sem("ring_lo")
        p_ready, p_saved = sem("p_ready"), sem("p_saved")
        pt_ready, s_ready = sem("pt_ready"), sem("s_ready")
        norms_step = sem("norms_step")
        sq_ready = sem("sq_ready")
        vec_ready = sem("vec_ready")
        inv_norm_ready = sem("inv_norm_ready")
        dvec_ready = sem("dvec_ready")
        rows_ready = sem("rows_ready")
        att_step = sem("att_step")
        dist_ready = sem("dist_ready")
        exp_done = sem("exp_done")
        k_ready = sem("k_ready")
        kt_ready, kt_hi_done, kt_lo_done = sem("kt_ready"), sem("kt_hi_done"), sem("kt_lo_done")
        o_ready, o_added = sem("o_ready"), sem("o_added")
        stats_ready, moments_ready = sem("stats_ready"), sem("moments_ready")
        var_ready = sem("var_ready")
        rstd_ready = sem("rstd_ready")
        shift_ready = sem("shift_ready")
        normed = sem("normed")

        def uses_to(i, use, last=False):
            return BEFORE + len(USES) * i + (LAST_USES if last else USES).index(use) + 1

        def bank_of(use, last=False):
            return ring[(LAST_USES if last else USES).index(use) % RING]

        def loads_of(g, parity):
            return DMA // 2 * (g - parity) + DMA

        def each_iteration(eng, body):
            body(0, 0, first=True)
            with eng.Fori(1, G - 2, 2) as i:
                body(i, 1)
                body(i + 1, 0)
            body(G - 1, 1, last=True)
            body(G, 0, tail=True)

        block = ctx.enter_context(nc.Block())

        @block.sync
        def _(sp):
            for k, w in (("lang", w_lang), ("grav", w_grav), ("o", w_o), ("v", w_v)):
                for c in range(C):
                    sp.dma_start(raw[k][:, c, :], weight_rows(w)[:, c, :]).then_inc(w_loaded[k][c], DMA)
            sp.dma_start(x_in[0][:], x_t[0]).then_inc(x_in_loaded[0], DMA)
            sp.wait_ge(w_hi["lang"], C)
            sp.wait_ge(w_lo["lang"], C)
            sp.dma_start(x_res[0][:], x_t[0]).then_inc(x_res_loaded[0], DMA)

            def body(i, parity, first=False, last=False, tail=False):
                if first:
                    sp.wait_ge(w_hi["grav"], C)
                    sp.wait_ge(w_lo["grav"], C)
                else:
                    for t in range(T):
                        sp.wait_ge(normed, T * (i - 1) + t + 1)
                        sp.dma_start(out_t[i - 1, :, t, :], x_res[1 - parity][:, t, :]).then_inc(stored, DMA)
                    sp.wait_ge(stored, DMA * T * i)
                if not last and not tail:
                    sp.dma_start(x_res[1 - parity][:], x_t[i + 1]).then_inc(x_res_loaded[1 - parity], DMA)

            each_iteration(sp, body)

        @block.gpsimd
        def _(pool):
            n = [0]

            def ordered(ins):
                n[0] += 1
                ins.then_inc(pool_step, 1)
                pool.wait_ge(pool_step, n[0])

            ordered(nc.gpsimd.memset(ident[:], 0.0))
            ordered(nc.gpsimd.affine_select(out=ident[:], in_=ident[:], compare_op=ALU.not_equal, fill=1.0,
                                            base=0, pattern=[[-1, P]], channel_multiplier=1))
            nc.gpsimd.engine_nop().then_inc(ident_ready, 1)
            ordered(nc.gpsimd.memset(half_ones[:], 0.0))
            ordered(nc.gpsimd.memset(half_ones[0:N, 0:N], 1.0))
            ordered(nc.gpsimd.memset(half_ones[N:P, N:P], 1.0))
            ordered(nc.gpsimd.memset(k_sb[:], 0.0))
            ordered(nc.gpsimd.memset(neg_half[:], -0.5))
            ordered(nc.gpsimd.memset(numer[:], 0.0))
            ordered(nc.gpsimd.memset(eye2[:], 0.0))
            pool.wait_ge(small_loaded, 4 * DMA)
            for h in range(2):
                for buf, fill in ((eye2, 1.0), (mask2, 0.0)):
                    ordered(nc.gpsimd.affine_select(
                        out=buf[:], in_=buf[:], compare_op=ALU.not_equal, fill=fill, base=-N * h,
                        pattern=[[-1, N]], channel_multiplier=1))
            nc.gpsimd.engine_nop().then_inc(consts_ready, 1)

            def body(i, parity, first=False, last=False, tail=False):
                if not first:
                    pool.wait_ge(var_ready, i)
                    nc.gpsimd.tensor_tensor(rstd[:], var_eps[:], neg_half[:, 0:T],
                                            ALU.pow).then_inc(rstd_ready, 1)
                if not tail:
                    pool.wait_ge(sq_ready, i + 1)
                    nc.gpsimd.tensor_tensor(vec[:, 0, :], sq_clamped[:], neg_half[:, 0:T],
                                            ALU.pow).then_inc(inv_norm_ready, 1)

            each_iteration(pool, body)

        @block.scalar
        def _(act):
            for h in range(2):
                act.dma_start(mask2[h * N:(h + 1) * N, :], adj).then_inc(small_loaded, DMA)
            with nc.allow_non_contiguous_dma(reason="two scalars"):
                act.dma_start(gates[:, 0:1], gate_logit.to_broadcast([P, 1])).then_inc(small_loaded, DMA)
                act.dma_start(gates[:, 1:2], log_sigma.to_broadcast([P, 1])).then_inc(small_loaded, DMA)

            def weight_hi(k):
                for c in range(C):
                    act.wait_ge(w_loaded[k][c], DMA)
                    nc.scalar.copy(split[k][0][:, c, :], raw[k][:, c, :]).then_inc(w_hi[k], 1)

            def hi_of_bank(dst, src, n):
                act.wait_ge(ring_ready, n)
                nc.scalar.copy(dst, src).then_inc(ring_hi, 1)

            def triangle_hi(k, r):
                n = C * k + r
                act.wait_ge(ring_ready, n + 1)
                done = nc.scalar.mul(tri_hi[:, k, row_start[r], :], ring[n % RING][:, 0:P], 0.5)
                if r < C - 1:
                    done = nc.scalar.copy(
                        tri_hi[:, k, row_start[r] + 1:row_start[r] + C - r, :].rearrange("p b d -> p (b d)"),
                        ring[n % RING][:, P:(C - r) * P])
                done.then_inc(ring_hi, 1)

            weight_hi("lang")
            act.wait_ge(small_loaded, 4 * DMA)
            nc.scalar.activation(gates[:, 2:3], gates[:, 0:1], ACT.Exp, scale=-1.0).then_inc(exps_ready, 1)
            nc.scalar.activation(gates[:, 5:6], gates[:, 1:2], ACT.Exp).then_inc(exps_ready, 1)
            weight_hi("grav")
            for r in range(C):
                triangle_hi(LANG, r)
            weight_hi("v")
            for r in range(C):
                triangle_hi(GRAV, r)
            for stage, dst in enumerate((wo_t_hi, wvo_hi, xt_hi[0])):
                for c in range(C):
                    n = (2 + stage) * C + c
                    hi_of_bank(dst[:, c, :], ring[n % RING][:], n + 1)

            def body(i, parity, first=False, last=False, tail=False):
                main, finish = not tail, not first
                uses = LAST_USES if last else USES
                if main and not last:
                    if first:
                        act.wait_ge(w_hi["v"], C)
                        act.wait_ge(w_lo["v"], C)
                    act.dma_start(x_in[1 - parity][:], x_t[i + 1]).then_inc(x_in_loaded[1 - parity], DMA)

                def take_hi(*use):
                    if main and use in uses:
                        dst = {"y": lambda k, c: y_hi[:, c, k, :], "x": lambda c: xt_hi[1 - parity][:, c, :],
                               "u": lambda t: u_hi[parity][:, t, :]}[use[0]](*use[1:])
                        hi_of_bank(dst, bank_of(use, last)[:], uses_to(i, use, last))

                def save_p(pair):
                    if main:
                        act.wait_ge(p_ready, PAIRS * i + pair + 1)
                        if not first:
                            act.wait_ge(s_ready, PAIRS * (i - 1) + pair + 1)
                        nc.scalar.copy(p_sb[:, pair].rearrange("p a k m -> p (a k m)"),
                                       p_bank[:]).then_inc(p_saved, 1)

                take_hi("y", LANG, 3)
                take_hi("y", LANG, 2)
                if finish:
                    act.wait_ge(dist_ready, i)
                    nc.scalar.activation(att[:, 1], att[:, 1], ACT.Exp, scale=neg_inv_two_var).then_inc(exp_done, 1)
                take_hi("y", GRAV, 3)
                take_hi("x", 0)
                take_hi("y", GRAV, 2)
                take_hi("x", 1)
                take_hi("y", LANG, 1)
                take_hi("x", 2)
                take_hi("y", GRAV, 1)
                take_hi("x", 3)
                take_hi("y", LANG, 0)
                take_hi("y", GRAV, 0)
                if finish:
                    act.wait_ge(kt_ready, i)
                    nc.scalar.copy(kt_hi[:].rearrange("p t n -> p (t n)"), rk_bank[:]).then_inc(kt_hi_done, 1)
                take_hi("u", 0)
                save_p(0)
                take_hi("u", 1)
                save_p(1)
                take_hi("u", 2)
                take_hi("u", 3)
                if finish:
                    act.wait_ge(shift_ready, i)
                    for t in range(T):
                        nc.scalar.activation(
                            x_res[1 - parity][:, t, :], x_res[1 - parity][:, t, :], ACT.Identity,
                            scale=rstd[:, t:t + 1], bias=shift[:, t:t + 1]).then_inc(normed, 1)

            each_iteration(act, body)

        @block.vector
        def _(dve):
            def weight_lo(k):
                for c in range(C):
                    dve.wait_ge(w_hi[k], c + 1)
                    nc.vector.tensor_sub(split[k][1][:, c, :], raw[k][:, c, :],
                                         split[k][0][:, c, :]).then_inc(w_lo[k], 1)

            def lo_of_bank(dst, src, hi, n):
                dve.wait_ge(ring_hi, n)
                nc.vector.tensor_sub(dst, src, hi).then_inc(ring_lo, 1)

            def triangle_lo(k, r):
                n = C * k + r
                dve.wait_ge(ring_hi, n + 1)
                done = nc.vector.scalar_tensor_tensor(
                    tri_lo[:, k, row_start[r], :], ring[n % RING][:, 0:P], 0.5, tri_hi[:, k, row_start[r], :],
                    ALU.mult, ALU.subtract)
                if r < C - 1:
                    rest = slice(row_start[r] + 1, row_start[r] + C - r)
                    done = nc.vector.tensor_sub(
                        tri_lo[:, k, rest, :].rearrange("p b d -> p (b d)"), ring[n % RING][:, P:(C - r) * P],
                        tri_hi[:, k, rest, :].rearrange("p b d -> p (b d)"))
                done.then_inc(ring_lo, 1)

            weight_lo("lang")
            dve.wait_ge(exps_ready, 2)
            nc.vector.tensor_scalar_add(gates[:, 3:4], gates[:, 2:3], 1.0)
            nc.vector.tensor_scalar(gates[:, 6:7], gates[:, 5:6], gates[:, 5:6], 2.0, ALU.mult,
                                    ALU.mult).then_inc(gates_step, 1)
            dve.wait_ge(gates_step, 1)
            nc.vector.reciprocal(gates[:, 3:4], gates[:, 3:4])
            nc.vector.reciprocal(gates[:, 7:8], gates[:, 6:7]).then_inc(gates_step, 1)
            dve.wait_ge(gates_step, 2)
            nc.vector.tensor_scalar(gates[:, 4:5], gates[:, 3:4], -1.0, 1.0, ALU.mult, ALU.add)
            nc.vector.tensor_scalar_mul(gates[:, 7:8], gates[:, 7:8], -1.0).then_inc(gates_step, 1)
            dve.wait_ge(gates_step, 3)
            dve.wait_ge(consts_ready, 1)
            nc.vector.tensor_scalar(numer[:, 1, :], numer[:, 1, :], w_grav_gate, None,
                                    ALU.add).then_inc(gates_ready, 1)

            weight_lo("grav")
            for r in range(C):
                triangle_lo(LANG, r)
            weight_lo("v")
            for r in range(C):
                triangle_lo(GRAV, r)
            for stage, (hi, lo) in enumerate(((wo_t_hi, wo_t_lo), (wvo_hi, wvo_lo), (xt_hi[0], xt_lo[0]))):
                for c in range(C):
                    n = (2 + stage) * C + c
                    lo_of_bank(lo[:, c, :], ring[n % RING][:], hi[:, c, :], n + 1)

            NORMS, ATT = 2, 10

            def body(i, parity, first=False, last=False, tail=False):
                main, finish = not tail, not first
                uses = LAST_USES if last else USES

                def stage(step, per_group, group):
                    n = [0]

                    def after(ins):
                        n[0] += 1
                        assert n[0] <= per_group
                        ins.then_inc(step, 1)
                        dve.wait_ge(step, per_group * group + n[0])
                    return after

                def take_lo(*use):
                    if main and use in uses:
                        hi, lo = {"y": lambda k, c: (y_hi[:, c, k, :], y_lo[:, c, k, :]),
                                  "x": lambda c: (xt_hi[1 - parity][:, c, :], xt_lo[1 - parity][:, c, :]),
                                  "u": lambda t: (u_hi[parity][:, t, :], u_lo[parity][:, t, :])}[use[0]](*use[1:])
                        lo_of_bank(lo, bank_of(use, last)[:], hi, uses_to(i, use, last))

                def add_transposed(pair):
                    if main:
                        dve.wait_ge(pt_ready, PAIRS * i + pair + 1)
                        for h in range(2):
                            rows, cols = slice(h * N, (h + 1) * N), slice(h * N, (h + 1) * N)
                            for a in range(2):
                                done = nc.vector.tensor_add(
                                    s_sb[rows, :, 2 * pair + a, :],
                                    pt_bank[rows, 2 * a * P:2 * (a + 1) * P].rearrange("p (k m) -> p k m", k=2)[:, :, cols],
                                    p_sb[rows, pair, a, :, cols])
                        done.then_inc(s_ready, 1)

                def norms():
                    if main:
                        after = stage(norms_step, NORMS, i)
                        dve.wait_ge(s_ready, PAIRS * (i + 1))
                        after(nc.vector.tensor_mul(
                            sdiag[:].rearrange("p k t m -> p (k t) m"), s_sb[:].rearrange("p k t m -> p (k t) m"),
                            eye2[:].unsqueeze(1).to_broadcast([P, 2 * T, N])))
                        after(nc.vector.reduce_sum(sq[:].rearrange("p k t -> p (k t)"),
                                                   sdiag[:].rearrange("p k t m -> p (k t) m"), AX_X))
                        nc.vector.tensor_scalar_max(sq_clamped[:], sq[:, 0, :], EPS * EPS).then_inc(sq_ready, 1)

                def spread_norms():
                    if finish:
                        nc.vector.tensor_copy(vec[:, 1, :], sq[:, 1, :]).then_inc(vec_ready, 1)
                        dve.wait_ge(vec_ready, i)
                        dve.wait_ge(inv_norm_ready, i)
                        nc.vector.tensor_scalar(numer[:, 0, :], vec[:, 0, :], w_lang_gate, None, ALU.mult)
                        nc.vector.tensor_mul(
                            dvec[:].rearrange("p k t m -> p (k t) m"),
                            eye2[:].unsqueeze(1).to_broadcast([P, 2 * T, N]),
                            vec[:].rearrange("p k t -> p (k t)").unsqueeze(2).to_broadcast([P, 2 * T, N]),
                        ).then_inc(dvec_ready, 1)

                after_att = stage(att_step, ATT, i - 1) if finish else None

                def distances():
                    if finish:
                        dve.wait_ge(rows_ready, i)
                        rows = rk_bank[:].rearrange("p (k t m) -> p k t m", k=2, t=T)
                        after_att(nc.vector.scalar_tensor_tensor(
                            att[:, 1], s_sb[:, 1], -2.0, rows[:, 1], ALU.mult, ALU.add))
                        after_att(nc.vector.tensor_add(
                            att[:, 1], att[:, 1], vec[:, 1, :].unsqueeze(2).to_broadcast([P, T, N])))
                        nc.vector.tensor_scalar_max(att[:, 1], att[:, 1], 0.0).then_inc(dist_ready, 1)
                        after_att(nc.vector.scalar_tensor_tensor(
                            att[:, 0], s_sb[:, 0], 0.0, rows[:, 0], ALU.max, ALU.mult))

                flat = att[:].rearrange("p k t m -> p (k t) m")

                def row_sums():
                    if finish:
                        dve.wait_ge(exp_done, i)
                        after_att(nc.vector.tensor_mul(flat, flat, mask2[:].unsqueeze(1).to_broadcast([P, 2 * T, N])))
                        after_att(nc.vector.reduce_sum(deg[:].rearrange("p k t -> p (k t)"), flat, AX_X))

                def row_scales():
                    if finish:
                        after_att(nc.vector.tensor_mul(deg[:, 0, :], deg[:, 0, :], vec[:, 0, :]))
                        after_att(nc.vector.tensor_scalar_max(deg_clamped[:], deg[:], EPS))
                        after_att(nc.vector.reciprocal(deg_inv[:], deg_clamped[:]))
                        after_att(nc.vector.tensor_mul(row_scale[:], deg_inv[:], numer[:]))

                def mix_kernels():
                    if finish:
                        after_att(nc.vector.tensor_mul(
                            flat, flat, row_scale[:].rearrange("p k t -> p (k t)").unsqueeze(2).to_broadcast([P, 2 * T, N])))
                        for h in range(2):
                            rows = slice(h * N, (h + 1) * N)
                            done = nc.vector.tensor_add(k_sb[rows, :, h * N:(h + 1) * N], att[rows, 0], att[rows, 1])
                        done.then_inc(k_ready, 1)

                def add_residual(t):
                    if finish:
                        if t == 0:
                            dve.wait_ge(x_res_loaded[1 - parity], loads_of(i - 1, 1 - parity))
                        dve.wait_ge(o_ready, T * (i - 1) + t + 1)
                        r = x_res[1 - parity][:, t, :]
                        nc.vector.tensor_add(r, o_bank[:], r).then_inc(o_added, 1)

                def layer_stats(t):
                    if finish:
                        dve.wait_ge(o_added, T * (i - 1) + t + 1)
                        nc.vector.bn_stats(stats[:, t, :], x_res[1 - parity][:, t, :]).then_inc(stats_ready, 1)

                def wait_for_stats():
                    if finish:
                        dve.wait_ge(stats_ready, T * i)

                def layer_moments():
                    if finish:
                        for t in range(T):
                            nc.vector.bn_aggr(mean_var[:, t, :], stats[:, t, :]).then_inc(moments_ready, 1)
                        dve.wait_ge(moments_ready, T * i)
                        nc.vector.tensor_scalar_add(var_eps[:], mean_var[:, :, 1], LN_EPS).then_inc(var_ready, 1)

                def layer_shift():
                    if finish:
                        dve.wait_ge(rstd_ready, i)
                        nc.vector.scalar_tensor_tensor(shift[:], mean_var[:, :, 0], -1.0, rstd[:],
                                                       ALU.mult, ALU.mult).then_inc(shift_ready, 1)

                spread_norms()
                take_lo("y", LANG, 3)
                take_lo("y", LANG, 2)
                distances()
                row_sums()
                take_lo("y", GRAV, 3)
                take_lo("x", 0)
                row_scales()
                take_lo("y", GRAV, 2)
                mix_kernels()
                take_lo("x", 1)
                take_lo("y", LANG, 1)
                take_lo("x", 2)
                take_lo("y", GRAV, 1)
                take_lo("x", 3)
                take_lo("y", LANG, 0)
                take_lo("y", GRAV, 0)
                if finish:
                    dve.wait_ge(kt_hi_done, i)
                    nc.vector.tensor_sub(kt_lo[:].rearrange("p t n -> p (t n)"), rk_bank[:],
                                         kt_hi[:].rearrange("p t n -> p (t n)")).then_inc(kt_lo_done, 1)
                add_residual(0)
                take_lo("u", 0)
                layer_stats(0)
                add_residual(1)
                take_lo("u", 1)
                add_transposed(0)
                add_residual(2)
                layer_stats(1)
                layer_stats(2)
                add_residual(3)
                take_lo("u", 2)
                layer_stats(3)
                wait_for_stats()
                add_transposed(1)
                layer_moments()
                norms()
                layer_shift()
                take_lo("u", 3)

            each_iteration(dve, body)

        @block.tensor
        def _(pe):
            def transpose_chunk(bank_, src, c):
                for t in range(T):
                    last = nc.tensor.transpose(bank_[:, t * P:(t + 1) * P], src[:, t, c * P:(c + 1) * P], ident[:])
                last.then_inc(ring_ready, 1)

            def product(dst, terms):
                for n, (lhs_t, rhs) in enumerate(terms):
                    last = nc.tensor.matmul(dst, lhs_t, rhs, start=n == 0, stop=n == len(terms) - 1)
                return last

            def three(a_hi, a_lo, b_hi, b_lo):
                return [(a_hi, b_hi), (a_hi, b_lo), (a_lo, b_hi)]

            def wait_for_bank(n):
                pe.wait_ge(ring_lo, n - RING)

            for k, name in enumerate(("lang", "grav")):
                hi, lo = split[name]
                for r in range(C):
                    n = k * C + r
                    if n >= RING:
                        wait_for_bank(n + 1)
                    rows, cols = slice(r * P, (r + 1) * P), slice(r * P, D)
                    dst = ring[n % RING][:, 0:D - r * P]
                    for c in range(C):
                        if r == 0:
                            pe.wait_ge(w_lo[name], c + 1)
                        for m, (a, b) in enumerate(three(hi[:, c, rows], lo[:, c, rows], hi[:, c, cols], lo[:, c, cols])):
                            done = nc.tensor.matmul(dst, a, b, start=c == m == 0, stop=c == C - 1 and m == 2)
                    done.then_inc(ring_ready, 1)
            pe.wait_ge(ident_ready, 1)
            for c in range(C):
                pe.wait_ge(w_loaded["o"][c], DMA)
            for c in range(C):
                wait_for_bank(2 * C + c + 1)
                transpose_chunk(ring[(2 * C + c) % RING], raw["o"], c)
            pe.wait_ge(w_lo["v"], C)
            pe.wait_ge(ring_lo, 3 * C)
            for r in range(C):
                n = 3 * C + r
                rows = slice(r * P, (r + 1) * P)
                terms = []
                for c in range(C):
                    terms += three(split["v"][0][:, c, rows], split["v"][1][:, c, rows], wo_t_hi[:, c, :], wo_t_lo[:, c, :])
                product(ring[n % RING][:], terms).then_inc(ring_ready, 1)
            pe.wait_ge(x_in_loaded[0], DMA)
            for c in range(C):
                wait_for_bank(4 * C + c + 1)
                transpose_chunk(ring[(4 * C + c) % RING], x_in[0], c)

            def body(i, parity, first=False, last=False, tail=False):
                main, finish = not tail, not first
                uses = LAST_USES if last else USES
                hi, lo = xt_hi[parity], xt_lo[parity]

                def fill(*use):
                    if not main or use not in uses:
                        return
                    n, dst = uses_to(i, use, last), bank_of(use, last)
                    wait_for_bank(n)
                    terms = []
                    if use[0] == "x":
                        if use[1] == 0:
                            pe.wait_ge(x_in_loaded[1 - parity], loads_of(i + 1, 1 - parity))
                        transpose_chunk(dst, x_in[1 - parity], use[1])
                        return
                    if use[0] == "y":
                        k, j = use[1:]
                        for r in range(j + 1):
                            b = block_of(r, j)
                            terms += three(tri_hi[:, k, b, :], tri_lo[:, k, b, :], hi[:, r, :], lo[:, r, :])
                    if use[0] == "u":
                        tok = slice(use[1] * P, (use[1] + 1) * P)
                        for c in range(C):
                            terms += three(hi[:, c, tok], lo[:, c, tok], wvo_hi[:, c, :], wvo_lo[:, c, :])
                    product(dst[:], terms).then_inc(ring_ready, 1)

                def inner_products(pair):
                    if main:
                        if pair == 0:
                            pe.wait_ge(ring_lo, uses_to(i, ("y", GRAV, 0), last))
                        for a in range(2):
                            tok = slice((2 * pair + a) * P, (2 * pair + a + 1) * P)
                            terms = []
                            for c in range(C):
                                terms += three(hi[:, c, tok], lo[:, c, tok], y_hi[:, c, :, tok], y_lo[:, c, :, tok])
                            done = product(p_bank[:, 2 * a * P:2 * (a + 1) * P].rearrange("p (k m) -> p k m", k=2), terms)
                        done.then_inc(p_ready, 1)

                def transpose_p(pair):
                    if main:
                        pe.wait_ge(p_saved, PAIRS * i + pair + 1)
                        if not first or pair:
                            pe.wait_ge(s_ready, PAIRS * i + pair)
                        for a in range(2):
                            for k in range(2):
                                b = 2 * a + k
                                done = nc.tensor.transpose(pt_bank[:, b * P:(b + 1) * P], p_sb[:, pair, a, k, :], ident[:])
                        done.then_inc(pt_ready, 1)

                def norms_along_rows():
                    if finish:
                        pe.wait_ge(dvec_ready, i)
                        nc.tensor.matmul(rk_bank[:], half_ones[:], dvec[:].rearrange("p k t m -> p (k t m)"),
                                         start=True, stop=True).then_inc(rows_ready, 1)

                def transpose_k():
                    if finish:
                        pe.wait_ge(k_ready, i)
                        for t in range(T):
                            done = nc.tensor.transpose(rk_bank[:, t * P:(t + 1) * P], k_sb[:, t, :], ident[:])
                        done.then_inc(kt_ready, 1)

                def attend(t):
                    if finish:
                        if t == 0:
                            pe.wait_ge(kt_lo_done, i)
                        else:
                            pe.wait_ge(o_added, T * (i - 1) + t)
                        product(o_bank[:], three(kt_hi[:, t, :], kt_lo[:, t, :], u_hi[1 - parity][:, t, :],
                                                 u_lo[1 - parity][:, t, :])).then_inc(o_ready, 1)

                if first:
                    pe.wait_ge(ring_lo, BEFORE)
                fill("y", LANG, 3)
                fill("y", LANG, 2)
                norms_along_rows()
                fill("y", GRAV, 3)
                fill("x", 0)
                fill("y", GRAV, 2)
                fill("x", 1)
                fill("y", LANG, 1)
                fill("x", 2)
                fill("y", GRAV, 1)
                fill("x", 3)
                fill("y", LANG, 0)
                fill("y", GRAV, 0)
                transpose_k()
                fill("u", 0)
                attend(0)
                inner_products(0)
                attend(1)
                fill("u", 1)
                transpose_p(0)
                attend(2)
                inner_products(1)
                attend(3)
                fill("u", 2)
                transpose_p(1)
                fill("u", 3)

            each_iteration(pe, body)


_INS = ["x", "adj", "L0_gnn_W_lang", "L0_gnn_W_grav", "L0_gnn_W_V", "L0_gnn_W_O", "L0_gnn_gate_logit",
        "L0_gnn_log_sigma"]
_OUTS = [((128, 64, 512), "float32")]


def kernel(**inputs):
    import numpy as _np
    import concourse.bacc as _bacc
    from concourse import mybir as _mybir
    from concourse.bass_utils import run_bass_kernel_spmd as _run

    nc = _bacc.Bacc("TRN2", target_bir_lowering=False, num_devices=1)
    arrays, args = {}, []
    for name in _INS:
        a = _np.ascontiguousarray(inputs[name])
        if a.ndim < 2:
            a = a.reshape(1, 1)
        arrays[f"in_{name}_dram"] = a
        args.append(nc.dram_tensor(f"in_{name}_dram", a.shape, _mybir.dt.from_np(a.dtype), kind="ExternalInput").ap())
    for i, (shape, dtype) in enumerate(_OUTS):
        dt = _mybir.dt.from_np(_np.dtype(dtype))
        args.append(nc.dram_tensor(f"out_{i}_dram", shape, dt, kind="ExternalOutput").ap())
    graph_attention_kernel(nc, *args)
    r = _run(nc, [arrays], core_ids=[0])
    got = tuple(r.results[0][f"out_{i}_dram"] for i in range(len(_OUTS)))
    return got[0]
```

```python
from contextlib import ExitStack

import concourse.bass as bass
from concourse import mybir

ALU = mybir.AluOpType
ACT = mybir.ActivationFunctionType
AX_X = mybir.AxisListType.X
F32 = mybir.dt.float32
F32R = mybir.dt.float32r

P = 128
EPS = 1e-8
LN_EPS = 1e-5
DMA = 16


def graph_attention_kernel(
    nc: bass.Bass,
    x: bass.AP,
    adj: bass.AP,
    w_lang: bass.AP,
    w_grav: bass.AP,
    w_v: bass.AP,
    w_o: bass.AP,
    gate_logit: bass.AP,
    log_sigma: bass.AP,
    out: bass.AP,
):
    B, N, D = x.shape
    C = D // P
    T = 4
    GT = T * P
    G = B * N // GT
    PAIRS = T // 2
    assert 2 * N == P and D == 512 and B * N == G * GT and G % 2 == 0

    row_start = [sum(C - r for r in range(i)) for i in range(C)]
    BLOCKS = C * (C + 1) // 2

    def block_of(i, j):
        return row_start[i] + j - i

    LANG, GRAV = 0, 1
    USES = [("y", LANG, 3), ("y", LANG, 2), ("y", GRAV, 3), ("x", 0), ("y", GRAV, 2), ("x", 1),
            ("y", LANG, 1), ("x", 2), ("y", GRAV, 1), ("y", LANG, 0), ("y", GRAV, 0), ("u", 0),
            ("x", 3), ("u", 1), ("u", 2), ("u", 3)]
    LAST_USES = [use for use in USES if use[0] != "x"]
    LATE_USES = [("u", 3)]
    RING = 4
    LANG_AT, W_O_AT, GRAV_AT, X_AT, W_VO_AT = (C * n for n in range(5))
    BEFORE = 5 * C
    assert len(USES) % RING == 0 and BEFORE % RING == 0

    x_t = x.rearrange("b n d -> (b n) d").rearrange("(g t p) d -> g p t d", t=T, p=P)
    out_t = out.rearrange("b n d -> (b n) d").rearrange("(g t p) d -> g p t d", t=T, p=P)

    def weight_rows(w):
        return w.rearrange("(c p) d -> p c d", p=P)

    with ExitStack() as ctx:
        def sb(name, shape, dt=F32):
            return ctx.enter_context(nc.sbuf_tensor(name, shape, dt))

        def bank(name):
            return ctx.enter_context(nc.psum_tensor(name, [P, 512], F32))

        def sem(name):
            return ctx.enter_context(nc.semaphore(name))

        ident = sb("ident", [P, P])
        eye2 = sb("eye2", [P, N])
        half_ones = sb("half_ones", [P, P], F32R)
        mask2 = sb("mask2", [P, N])
        neg_half = sb("neg_half", [P, 2 * T])
        gates = sb("gates", [P, 8])
        w_lang_gate, w_grav_gate, neg_inv_two_var = gates[:, 3:4], gates[:, 4:5], gates[:, 7:8]

        tri_hi = sb("tri_hi", [P, 2, BLOCKS, P], F32R)
        tri_lo = sb("tri_lo", [P, 2, BLOCKS, P], F32R)
        wvo_hi = sb("wvo_hi", [P, C, D], F32R)
        wvo_lo = sb("wvo_lo", [P, C, D], F32R)

        x_in = [sb(f"x_in{i}", [P, T, D]) for i in range(2)]
        x_res = [sb(f"x_res{i}", [P, T, D]) for i in range(2)]
        xt_hi = [sb(f"xt_hi{i}", [P, C, GT], F32R) for i in range(2)]
        xt_lo = [sb(f"xt_lo{i}", [P, C, GT], F32R) for i in range(2)]
        y_hi = sb("y_hi", [P, C, 2, GT], F32R)
        y_lo = sb("y_lo", [P, C, 2, GT], F32R)
        u_hi = [sb(f"u_hi{i}", [P, T, D], F32R) for i in range(2)]
        u_lo = [sb(f"u_lo{i}", [P, T, D], F32R) for i in range(2)]

        raw = {"lang": x_res[0], "grav": x_res[1], "v": x_in[1], "o": sb("w_o_raw", [P, C, D])}
        split = {
            "lang": (y_hi[:, :, 0, :], y_lo[:, :, 0, :]),
            "grav": (y_hi[:, :, 1, :], y_lo[:, :, 1, :]),
            "v": (xt_hi[1], xt_lo[1]),
        }
        wo_t_hi, wo_t_lo = u_hi[0], u_lo[0]

        p_sb = sb("p_sb", [P, PAIRS, 2, 2, P])
        s_sb = sb("s_sb", [P, 2, T, N])
        sdiag = sb("sdiag", [P, 2, T, N])
        sq = sb("sq", [P, 2, T])
        sq_clamped = sb("sq_clamped", [P, T])
        vec = sb("vec", [P, 2, T])
        numer = sb("numer", [P, 2, T])
        vec_hi = sb("vec_hi", [P, 2, T], F32R)
        vec_lo = sb("vec_lo", [P, 2, T])
        dvec_hi = sb("dvec_hi", [P, 2, T, N], F32R)
        dvec_lo = sb("dvec_lo", [P, 2, T, N], F32R)
        att = sb("att", [P, 2, T, N])
        deg = sb("deg", [P, 2, T])
        deg_clamped = sb("deg_clamped", [P, 2, T])
        deg_inv = sb("deg_inv", [P, 2, T])
        row_scale = sb("row_scale", [P, 2, T])
        k_sb = sb("k_sb", [P, T, P])
        kt_hi = sb("kt_hi", [P, T, P], F32R)
        kt_lo = sb("kt_lo", [P, T, P], F32R)
        stats = sb("stats", [P, T, 6])
        mean_var = sb("mean_var", [P, T, 2])
        var_eps = sb("var_eps", [P, T])
        rstd = sb("rstd", [P, T])
        shift = sb("shift", [P, T])

        ring = [bank(f"ring{i}") for i in range(RING)]
        p_bank = bank("p_bank")
        pt_bank = bank("pt_bank")
        rk_bank = bank("rk_bank")
        o_bank = bank("o_bank")

        w_loaded = {k: [sem(f"w_{k}_loaded{c}") for c in range(C)] for k in ("lang", "grav", "v", "o")}
        w_hi = {k: sem(f"w_{k}_hi") for k in split}
        w_lo = {k: sem(f"w_{k}_lo") for k in split}
        small_loaded = sem("small_loaded")
        ident_ready = sem("ident_ready")
        consts_ready = sem("consts_ready")
        pool_step = sem("pool_step")
        exps_ready = sem("exps_ready")
        gates_step = sem("gates_step")
        gates_ready = sem("gates_ready")
        x_in_loaded = [sem(f"x_in_loaded{i}") for i in range(2)]
        x_res_loaded = [sem(f"x_res_loaded{i}") for i in range(2)]
        stored = sem("stored")
        ring_ready, ring_hi, ring_lo = sem("ring_ready"), sem("ring_hi"), sem("ring_lo")
        p_ready, p_saved = sem("p_ready"), sem("p_saved")
        pt_ready, s_ready = sem("pt_ready"), sem("s_ready")
        norms_step = sem("norms_step")
        sq_ready = sem("sq_ready")
        vec_hi_step, vec_lo_ready = sem("vec_hi_step"), sem("vec_lo_ready")
        inv_norm_ready = sem("inv_norm_ready")
        dvec_ready = sem("dvec_ready")
        rows_ready = sem("rows_ready")
        att_step = sem("att_step")
        dist_ready = sem("dist_ready")
        exp_done = sem("exp_done")
        k_ready = sem("k_ready")
        kt_ready, kt_hi_done, kt_lo_done = sem("kt_ready"), sem("kt_hi_done"), sem("kt_lo_done")
        o_ready, o_added = sem("o_ready"), sem("o_added")
        stats_ready, moments_ready = sem("stats_ready"), sem("moments_ready")
        var_ready = sem("var_ready")
        rstd_ready = sem("rstd_ready")
        shift_ready = sem("shift_ready")
        normed = sem("normed")

        def uses_to(i, use, last=False):
            return BEFORE + len(USES) * i + (LAST_USES if last else USES).index(use) + 1

        def bank_of(use, last=False):
            return ring[(LAST_USES if last else USES).index(use) % RING]

        def o_bank_of(t, tail):
            return (o_bank, p_bank, pt_bank, o_bank)[t] if tail else o_bank

        def loads_of(g, parity):
            return DMA // 2 * (g - parity) + DMA

        def each_iteration(eng, body):
            body(0, 0, first=True)
            with eng.Fori(1, G - 2, 2) as i:
                body(i, 1)
                body(i + 1, 0)
            body(G - 1, 1, last=True)
            body(G, 0, tail=True)

        block = ctx.enter_context(nc.Block())

        @block.sync
        def _(sp):
            for k, w in (("lang", w_lang), ("o", w_o), ("grav", w_grav), ("v", w_v)):
                for c in range(C):
                    sp.dma_start(raw[k][:, c, :], weight_rows(w)[:, c, :]).then_inc(w_loaded[k][c], DMA)
            sp.dma_start(x_in[0][:], x_t[0]).then_inc(x_in_loaded[0], DMA)
            sp.wait_ge(w_hi["lang"], C)
            sp.wait_ge(w_lo["lang"], C)
            sp.dma_start(x_res[0][:], x_t[0]).then_inc(x_res_loaded[0], DMA)

            def body(i, parity, first=False, last=False, tail=False):
                if first:
                    sp.wait_ge(w_hi["grav"], C)
                    sp.wait_ge(w_lo["grav"], C)
                else:
                    for t in range(T):
                        sp.wait_ge(normed, T * (i - 1) + t + 1)
                        sp.dma_start(out_t[i - 1, :, t, :], x_res[1 - parity][:, t, :]).then_inc(stored, DMA)
                    sp.wait_ge(stored, DMA * T * i)
                if not last and not tail:
                    sp.dma_start(x_res[1 - parity][:], x_t[i + 1]).then_inc(x_res_loaded[1 - parity], DMA)

            each_iteration(sp, body)

        @block.gpsimd
        def _(pool):
            n = [0]

            def ordered(ins):
                n[0] += 1
                ins.then_inc(pool_step, 1)
                pool.wait_ge(pool_step, n[0])

            ordered(nc.gpsimd.memset(ident[:], 0.0))
            ordered(nc.gpsimd.affine_select(out=ident[:], in_=ident[:], compare_op=ALU.not_equal, fill=1.0,
                                            base=0, pattern=[[-1, P]], channel_multiplier=1))
            nc.gpsimd.engine_nop().then_inc(ident_ready, 1)
            ordered(nc.gpsimd.memset(half_ones[:].bitcast(F32), 0.0))
            ordered(nc.gpsimd.memset(half_ones[0:N, 0:N].bitcast(F32), 1.0))
            ordered(nc.gpsimd.memset(half_ones[N:P, N:P].bitcast(F32), 1.0))
            ordered(nc.gpsimd.memset(k_sb[:], 0.0))
            ordered(nc.gpsimd.memset(neg_half[:], -0.5))
            ordered(nc.gpsimd.memset(numer[:], 0.0))
            ordered(nc.gpsimd.memset(eye2[:], 0.0))
            pool.wait_ge(small_loaded, 4 * DMA)
            for h in range(2):
                for buf, fill in ((eye2, 1.0), (mask2, 0.0)):
                    ordered(nc.gpsimd.affine_select(
                        out=buf[:], in_=buf[:], compare_op=ALU.not_equal, fill=fill, base=-N * h,
                        pattern=[[-1, N]], channel_multiplier=1))
            nc.gpsimd.engine_nop().then_inc(consts_ready, 1)

            def inverse_norms(g):
                pool.wait_ge(sq_ready, g + 1)
                nc.gpsimd.tensor_tensor(vec[:, 0, :], sq_clamped[:], neg_half[:, 0:T],
                                        ALU.pow).then_inc(inv_norm_ready, 1)

            def body(i, parity, first=False, last=False, tail=False):
                if last:
                    inverse_norms(i)
                if not first:
                    step = 1 if tail else T
                    for t in range(0, T, step):
                        pool.wait_ge(var_ready, i + t)
                        nc.gpsimd.tensor_tensor(rstd[:, t:t + step], var_eps[:, t:t + step], neg_half[:, 0:step],
                                                ALU.pow).then_inc(rstd_ready, 1)
                if not tail and not last:
                    inverse_norms(i)

            each_iteration(pool, body)

        @block.scalar
        def _(act):
            for h in range(2):
                act.dma_start(mask2[h * N:(h + 1) * N, :], adj).then_inc(small_loaded, DMA)
            with nc.allow_non_contiguous_dma(reason="two scalars"):
                act.dma_start(gates[:, 0:1], gate_logit.to_broadcast([P, 1])).then_inc(small_loaded, DMA)
                act.dma_start(gates[:, 1:2], log_sigma.to_broadcast([P, 1])).then_inc(small_loaded, DMA)

            def weight_hi(k):
                for c in range(C):
                    act.wait_ge(w_loaded[k][c], DMA)
                    nc.scalar.copy(split[k][0][:, c, :], raw[k][:, c, :]).then_inc(w_hi[k], 1)

            def hi_of_bank(dst, src, n):
                act.wait_ge(ring_ready, n)
                nc.scalar.copy(dst, src).then_inc(ring_hi, 1)

            def triangle_hi(k, r):
                n = (LANG_AT, GRAV_AT)[k] + r
                act.wait_ge(ring_ready, n + 1)
                done = nc.scalar.mul(tri_hi[:, k, row_start[r], :], ring[n % RING][:, 0:P], 0.5)
                if r < C - 1:
                    done = nc.scalar.copy(
                        tri_hi[:, k, row_start[r] + 1:row_start[r] + C - r, :].rearrange("p b d -> p (b d)"),
                        ring[n % RING][:, P:(C - r) * P])
                done.then_inc(ring_hi, 1)

            weight_hi("lang")
            act.wait_ge(small_loaded, 4 * DMA)
            nc.scalar.activation(gates[:, 2:3], gates[:, 0:1], ACT.Exp, scale=-1.0).then_inc(exps_ready, 1)
            nc.scalar.activation(gates[:, 5:6], gates[:, 1:2], ACT.Exp).then_inc(exps_ready, 1)
            weight_hi("grav")

            def stage_hi(at, dst):
                for c in range(C):
                    hi_of_bank(dst[:, c, :], ring[(at + c) % RING][:], at + c + 1)

            for r in range(C):
                triangle_hi(LANG, r)
            stage_hi(W_O_AT, wo_t_hi)
            weight_hi("v")
            for r in range(C):
                triangle_hi(GRAV, r)
            stage_hi(X_AT, xt_hi[0])
            stage_hi(W_VO_AT, wvo_hi)

            def body(i, parity, first=False, last=False, tail=False):
                main, finish = not tail, not first
                uses = LATE_USES if tail else LAST_USES if last else USES
                g, par, ends = (i - 1, 1 - parity, True) if tail else (i, parity, last)
                if main and not last:
                    if first:
                        act.wait_ge(w_hi["v"], C)
                        act.wait_ge(w_lo["v"], C)
                    act.dma_start(x_in[1 - parity][:], x_t[i + 1]).then_inc(x_in_loaded[1 - parity], DMA)

                def take_hi(*use):
                    if use in uses:
                        dst = {"y": lambda k, c: y_hi[:, c, k, :], "x": lambda c: xt_hi[1 - parity][:, c, :],
                               "u": lambda t: u_hi[par][:, t, :]}[use[0]](*use[1:])
                        hi_of_bank(dst, bank_of(use, ends)[:], uses_to(g, use, ends))

                def save_p(pair):
                    if main:
                        act.wait_ge(p_ready, T * i + 2 * pair + 2)
                        if not first:
                            act.wait_ge(s_ready, PAIRS * (i - 1) + pair + 1)
                        nc.scalar.copy(p_sb[:, pair].rearrange("p a k m -> p (a k m)"),
                                       p_bank[:]).then_inc(p_saved, 1)

                def scale_and_shift(buf, t):
                    nc.scalar.activation(buf[:, t, :], buf[:, t, :], ACT.Identity,
                                         scale=rstd[:, t:t + 1], bias=shift[:, t:t + 1]).then_inc(normed, 1)

                def normalize(t):
                    if finish:
                        if t == 0 or tail:
                            act.wait_ge(shift_ready, i + t)
                        scale_and_shift(x_res[1 - parity], t)

                take_hi("y", LANG, 3)
                take_hi("y", LANG, 2)
                if finish:
                    act.wait_ge(dist_ready, i)
                    nc.scalar.activation(att[:, 1], att[:, 1], ACT.Exp, scale=neg_inv_two_var).then_inc(exp_done, 1)
                if tail:
                    take_hi("u", 3)
                    act.wait_ge(shift_ready, i - 1)
                    for t in range(T):
                        scale_and_shift(x_res[parity], t)
                take_hi("y", GRAV, 3)
                take_hi("x", 0)
                take_hi("y", GRAV, 2)
                take_hi("x", 1)
                take_hi("y", LANG, 1)
                take_hi("x", 2)
                take_hi("y", GRAV, 1)
                take_hi("y", LANG, 0)
                take_hi("y", GRAV, 0)
                take_hi("u", 0)
                if finish:
                    act.wait_ge(kt_ready, i)
                    nc.scalar.copy(kt_hi[:].rearrange("p t n -> p (t n)"), rk_bank[:]).then_inc(kt_hi_done, 1)
                take_hi("x", 3)
                save_p(0)
                if not last:
                    take_hi("u", 1)
                    save_p(1)
                    normalize(0)
                    take_hi("u", 2)
                    normalize(1)
                    normalize(2)
                    normalize(3)
                    if main:
                        take_hi("u", 3)
                else:
                    save_p(1)
                    take_hi("u", 1)
                    take_hi("u", 2)

            each_iteration(act, body)

        @block.vector
        def _(dve):
            def weight_lo(k):
                for c in range(C):
                    dve.wait_ge(w_hi[k], c + 1)
                    nc.vector.tensor_sub(split[k][1][:, c, :], raw[k][:, c, :],
                                         split[k][0][:, c, :]).then_inc(w_lo[k], 1)

            def lo_of_bank(dst, src, hi, n):
                dve.wait_ge(ring_hi, n)
                nc.vector.tensor_sub(dst, src, hi).then_inc(ring_lo, 1)

            def triangle_lo(k, r):
                n = (LANG_AT, GRAV_AT)[k] + r
                dve.wait_ge(ring_hi, n + 1)
                done = nc.vector.scalar_tensor_tensor(
                    tri_lo[:, k, row_start[r], :], ring[n % RING][:, 0:P], 0.5, tri_hi[:, k, row_start[r], :],
                    ALU.mult, ALU.subtract)
                if r < C - 1:
                    rest = slice(row_start[r] + 1, row_start[r] + C - r)
                    done = nc.vector.tensor_sub(
                        tri_lo[:, k, rest, :].rearrange("p b d -> p (b d)"), ring[n % RING][:, P:(C - r) * P],
                        tri_hi[:, k, rest, :].rearrange("p b d -> p (b d)"))
                done.then_inc(ring_lo, 1)

            weight_lo("lang")
            dve.wait_ge(exps_ready, 2)
            nc.vector.tensor_scalar_add(gates[:, 3:4], gates[:, 2:3], 1.0)
            nc.vector.tensor_scalar(gates[:, 6:7], gates[:, 5:6], gates[:, 5:6], 2.0, ALU.mult,
                                    ALU.mult).then_inc(gates_step, 1)
            dve.wait_ge(gates_step, 1)
            nc.vector.reciprocal(gates[:, 3:4], gates[:, 3:4])
            nc.vector.reciprocal(gates[:, 7:8], gates[:, 6:7]).then_inc(gates_step, 1)
            dve.wait_ge(gates_step, 2)
            nc.vector.tensor_scalar(gates[:, 4:5], gates[:, 3:4], -1.0, 1.0, ALU.mult, ALU.add)
            nc.vector.tensor_scalar_mul(gates[:, 7:8], gates[:, 7:8], -1.0).then_inc(gates_step, 1)
            dve.wait_ge(gates_step, 3)
            dve.wait_ge(consts_ready, 1)
            nc.vector.tensor_scalar(numer[:, 1, :], numer[:, 1, :], w_grav_gate, None,
                                    ALU.add).then_inc(gates_ready, 1)

            weight_lo("grav")

            def stage_lo(at, hi, lo):
                for c in range(C):
                    lo_of_bank(lo[:, c, :], ring[(at + c) % RING][:], hi[:, c, :], at + c + 1)

            for r in range(C):
                triangle_lo(LANG, r)
            stage_lo(W_O_AT, wo_t_hi, wo_t_lo)
            weight_lo("v")
            for r in range(C):
                triangle_lo(GRAV, r)
            stage_lo(X_AT, xt_hi[0], xt_lo[0])
            stage_lo(W_VO_AT, wvo_hi, wvo_lo)

            NORMS, SPREAD, ATT = 2, 2, 10

            def body(i, parity, first=False, last=False, tail=False):
                main, finish = not tail, not first
                uses = LATE_USES if tail else LAST_USES if last else USES
                g, par, ends = (i - 1, 1 - parity, True) if tail else (i, parity, last)

                def stage(step, per_group, group):
                    n = [0]

                    def after(ins):
                        n[0] += 1
                        assert n[0] <= per_group
                        ins.then_inc(step, 1)
                        dve.wait_ge(step, per_group * group + n[0])
                    return after

                def take_lo(*use):
                    if use in uses:
                        hi, lo = {"y": lambda k, c: (y_hi[:, c, k, :], y_lo[:, c, k, :]),
                                  "x": lambda c: (xt_hi[1 - parity][:, c, :], xt_lo[1 - parity][:, c, :]),
                                  "u": lambda t: (u_hi[par][:, t, :], u_lo[par][:, t, :])}[use[0]](*use[1:])
                        lo_of_bank(lo, bank_of(use, ends)[:], hi, uses_to(g, use, ends))

                def add_transposed(pair):
                    if main:
                        dve.wait_ge(pt_ready, PAIRS * i + pair + 1)
                        for h in range(2):
                            rows, cols = slice(h * N, (h + 1) * N), slice(h * N, (h + 1) * N)
                            for a in range(2):
                                done = nc.vector.tensor_add(
                                    s_sb[rows, :, 2 * pair + a, :],
                                    pt_bank[rows, 2 * a * P:2 * (a + 1) * P].rearrange("p (k m) -> p k m", k=2)[:, :, cols],
                                    p_sb[rows, pair, a, :, cols])
                        done.then_inc(s_ready, 1)

                def norms():
                    if main:
                        after = stage(norms_step, NORMS, i)
                        dve.wait_ge(s_ready, PAIRS * (i + 1))
                        after(nc.vector.tensor_mul(
                            sdiag[:].rearrange("p k t m -> p (k t) m"), s_sb[:].rearrange("p k t m -> p (k t) m"),
                            eye2[:].unsqueeze(1).to_broadcast([P, 2 * T, N])))
                        after(nc.vector.reduce_sum(sq[:].rearrange("p k t -> p (k t)"),
                                                   sdiag[:].rearrange("p k t m -> p (k t) m"), AX_X))
                        nc.vector.tensor_scalar_max(sq_clamped[:], sq[:, 0, :], EPS * EPS).then_inc(sq_ready, 1)

                def spread_norms():
                    if main:
                        after = stage(vec_hi_step, SPREAD, i)

                        def on_diagonals(dst, v):
                            return nc.vector.tensor_mul(
                                dst[:].rearrange("p k t m -> p (k t) m"), eye2[:].unsqueeze(1).to_broadcast([P, 2 * T, N]),
                                v[:].rearrange("p k t -> p (k t)").unsqueeze(2).to_broadcast([P, 2 * T, N]))

                        after(nc.vector.tensor_copy(vec[:, 1, :], sq[:, 1, :]))
                        dve.wait_ge(inv_norm_ready, i + 1)
                        after(nc.vector.tensor_copy(vec_hi[:], vec[:]))
                        nc.vector.tensor_sub(vec_lo[:], vec[:], vec_hi[:]).then_inc(vec_lo_ready, 1)
                        on_diagonals(dvec_hi, vec)
                        dve.wait_ge(vec_lo_ready, i + 1)
                        on_diagonals(dvec_lo, vec_lo).then_inc(dvec_ready, 1)
                        nc.vector.tensor_scalar(numer[:, 0, :], vec[:, 0, :], w_lang_gate, None, ALU.mult)

                after_att = stage(att_step, ATT, i - 1) if finish else None

                def distances():
                    if finish:
                        dve.wait_ge(rows_ready, i)
                        rows = rk_bank[:].rearrange("p (k t m) -> p k t m", k=2, t=T)
                        after_att(nc.vector.scalar_tensor_tensor(
                            att[:, 1], s_sb[:, 1], -2.0, rows[:, 1], ALU.mult, ALU.add))
                        after_att(nc.vector.tensor_add(
                            att[:, 1], att[:, 1], vec[:, 1, :].unsqueeze(2).to_broadcast([P, T, N])))
                        nc.vector.tensor_scalar_max(att[:, 1], att[:, 1], 0.0).then_inc(dist_ready, 1)
                        after_att(nc.vector.scalar_tensor_tensor(
                            att[:, 0], s_sb[:, 0], 0.0, rows[:, 0], ALU.max, ALU.mult))

                flat = att[:].rearrange("p k t m -> p (k t) m")

                def row_sums():
                    if finish:
                        dve.wait_ge(exp_done, i)
                        after_att(nc.vector.tensor_mul(flat, flat, mask2[:].unsqueeze(1).to_broadcast([P, 2 * T, N])))
                        after_att(nc.vector.reduce_sum(deg[:].rearrange("p k t -> p (k t)"), flat, AX_X))

                def row_scales():
                    if finish:
                        after_att(nc.vector.tensor_mul(deg[:, 0, :], deg[:, 0, :], vec[:, 0, :]))
                        after_att(nc.vector.tensor_scalar_max(deg_clamped[:], deg[:], EPS))
                        after_att(nc.vector.reciprocal(deg_inv[:], deg_clamped[:]))
                        after_att(nc.vector.tensor_mul(row_scale[:], deg_inv[:], numer[:]))

                def scale_rows():
                    if finish:
                        after_att(nc.vector.tensor_mul(
                            flat, flat, row_scale[:].rearrange("p k t -> p (k t)").unsqueeze(2).to_broadcast([P, 2 * T, N])))

                def mix_kernels():
                    if finish:
                        for h in range(2):
                            rows = slice(h * N, (h + 1) * N)
                            done = nc.vector.tensor_add(k_sb[rows, :, h * N:(h + 1) * N], att[rows, 0], att[rows, 1])
                        done.then_inc(k_ready, 1)

                def add_residual(t):
                    if finish:
                        if t == 0:
                            dve.wait_ge(x_res_loaded[1 - parity], loads_of(i - 1, 1 - parity))
                        dve.wait_ge(o_ready, T * (i - 1) + t + 1)
                        r = x_res[1 - parity][:, t, :]
                        nc.vector.tensor_add(r, o_bank_of(t, tail)[:], r).then_inc(o_added, 1)

                def layer_stats(t):
                    if finish:
                        dve.wait_ge(o_added, T * (i - 1) + t + 1)
                        nc.vector.bn_stats(stats[:, t, :], x_res[1 - parity][:, t, :]).then_inc(stats_ready, 1)

                def wait_for_stats():
                    if finish:
                        dve.wait_ge(stats_ready, T * i)

                def layer_moments(t0=0, t1=T):
                    if finish:
                        for t in range(t0, t1):
                            nc.vector.bn_aggr(mean_var[:, t, :], stats[:, t, :]).then_inc(moments_ready, 1)
                        dve.wait_ge(moments_ready, T * (i - 1) + t1)
                        nc.vector.tensor_scalar_add(var_eps[:, t0:t1], mean_var[:, t0:t1, 1], LN_EPS).then_inc(var_ready, 1)

                def layer_shift(t0=0, t1=T):
                    if finish:
                        dve.wait_ge(rstd_ready, i + t0)
                        nc.vector.scalar_tensor_tensor(shift[:, t0:t1], mean_var[:, t0:t1, 0], -1.0, rstd[:, t0:t1],
                                                       ALU.mult, ALU.mult).then_inc(shift_ready, 1)

                take_lo("y", LANG, 3)
                distances()
                take_lo("y", LANG, 2)
                row_sums()
                if tail:
                    take_lo("u", 3)
                take_lo("y", GRAV, 3)
                take_lo("x", 0)
                row_scales()
                take_lo("y", GRAV, 2)
                take_lo("x", 1)
                scale_rows()
                take_lo("y", LANG, 1)
                take_lo("x", 2)
                mix_kernels()
                take_lo("y", GRAV, 1)
                take_lo("y", LANG, 0)
                take_lo("y", GRAV, 0)
                take_lo("u", 0)
                if finish:
                    dve.wait_ge(kt_hi_done, i)
                    nc.vector.tensor_sub(kt_lo[:].rearrange("p t n -> p (t n)"), rk_bank[:],
                                         kt_hi[:].rearrange("p t n -> p (t n)")).then_inc(kt_lo_done, 1)
                take_lo("x", 3)
                add_residual(0)
                layer_stats(0)
                if tail:
                    dve.wait_ge(stats_ready, T * (i - 1) + 1)
                    layer_moments(0, 1)
                    for t in range(1, T):
                        add_residual(t)
                        layer_stats(t)
                        dve.wait_ge(stats_ready, T * (i - 1) + t + 1)
                        layer_moments(t, t + 1)
                        layer_shift(t - 1, t)
                    layer_shift(T - 1, T)
                    return
                add_residual(1)
                layer_stats(1)
                if not last:
                    take_lo("u", 1)
                add_residual(2)
                layer_stats(2)
                if not last:
                    add_residual(3)
                    layer_stats(3)
                    wait_for_stats()
                    add_transposed(0)
                    layer_moments()
                    layer_shift()
                    add_transposed(1)
                    norms()
                    take_lo("u", 2)
                    spread_norms()
                    take_lo("u", 3)
                else:
                    add_transposed(0)
                    add_transposed(1)
                    norms()
                    add_residual(3)
                    layer_stats(3)
                    wait_for_stats()
                    spread_norms()
                    layer_moments()
                    take_lo("u", 1)
                    layer_shift()
                    take_lo("u", 2)

            each_iteration(dve, body)

        @block.tensor
        def _(pe):
            def transpose_chunk(bank_, src, c):
                for t in range(T):
                    last = nc.tensor.transpose(bank_[:, t * P:(t + 1) * P], src[:, t, c * P:(c + 1) * P], ident[:])
                last.then_inc(ring_ready, 1)

            def product(dst, terms):
                for n, (lhs_t, rhs) in enumerate(terms):
                    last = nc.tensor.matmul(dst, lhs_t, rhs, start=n == 0, stop=n == len(terms) - 1)
                return last

            def three(a_hi, a_lo, b_hi, b_lo):
                return [(a_hi, b_hi), (a_hi, b_lo), (a_lo, b_hi)]

            def wait_for_bank(n):
                pe.wait_ge(ring_lo, n - RING)

            def triangle(name, at):
                hi, lo = split[name]
                for r in range(C):
                    if at + r >= RING:
                        wait_for_bank(at + r + 1)
                    rows, cols = slice(r * P, (r + 1) * P), slice(r * P, D)
                    dst = ring[(at + r) % RING][:, 0:D - r * P]
                    for c in range(C):
                        if r == 0:
                            pe.wait_ge(w_lo[name], c + 1)
                        for m, (a, b) in enumerate(three(hi[:, c, rows], lo[:, c, rows], hi[:, c, cols], lo[:, c, cols])):
                            done = nc.tensor.matmul(dst, a, b, start=c == m == 0, stop=c == C - 1 and m == 2)
                    done.then_inc(ring_ready, 1)

            triangle("lang", LANG_AT)
            pe.wait_ge(ident_ready, 1)
            for c in range(C):
                pe.wait_ge(w_loaded["o"][c], DMA)
            for c in range(C):
                wait_for_bank(W_O_AT + c + 1)
                transpose_chunk(ring[(W_O_AT + c) % RING], raw["o"], c)
            triangle("grav", GRAV_AT)
            pe.wait_ge(x_in_loaded[0], DMA)
            for c in range(C):
                wait_for_bank(X_AT + c + 1)
                transpose_chunk(ring[(X_AT + c) % RING], x_in[0], c)
            pe.wait_ge(w_lo["v"], C)
            for r in range(C):
                n = W_VO_AT + r
                wait_for_bank(n + 1)
                rows = slice(r * P, (r + 1) * P)
                terms = []
                for c in range(C):
                    terms += three(split["v"][0][:, c, rows], split["v"][1][:, c, rows], wo_t_hi[:, c, :], wo_t_lo[:, c, :])
                product(ring[n % RING][:], terms).then_inc(ring_ready, 1)

            def body(i, parity, first=False, last=False, tail=False):
                main, finish = not tail, not first
                uses = LATE_USES if tail else LAST_USES if last else USES
                g, par, ends = (i - 1, 1 - parity, True) if tail else (i, parity, last)
                hi, lo = xt_hi[par], xt_lo[par]

                def fill(*use):
                    if use not in uses:
                        return
                    n, dst = uses_to(g, use, ends), bank_of(use, ends)
                    wait_for_bank(n)
                    terms = []
                    if use[0] == "x":
                        if use[1] == 0:
                            pe.wait_ge(x_in_loaded[1 - parity], loads_of(i + 1, 1 - parity))
                        transpose_chunk(dst, x_in[1 - parity], use[1])
                        return
                    if use[0] == "y":
                        k, j = use[1:]
                        for r in range(j + 1):
                            b = block_of(r, j)
                            terms += three(tri_hi[:, k, b, :], tri_lo[:, k, b, :], hi[:, r, :], lo[:, r, :])
                    if use[0] == "u":
                        if first and use[1] == 0:
                            pe.wait_ge(ring_lo, BEFORE)
                        tok = slice(use[1] * P, (use[1] + 1) * P)
                        for c in range(C):
                            terms += three(hi[:, c, tok], lo[:, c, tok], wvo_hi[:, c, :], wvo_lo[:, c, :])
                    product(dst[:], terms).then_inc(ring_ready, 1)

                def inner_products(t):
                    if main:
                        if t == 0:
                            pe.wait_ge(ring_lo, uses_to(i, ("y", GRAV, 0), last))
                        a = t % 2
                        tok = slice(t * P, (t + 1) * P)
                        terms = []
                        for c in range(C):
                            terms += three(hi[:, c, tok], lo[:, c, tok], y_hi[:, c, :, tok], y_lo[:, c, :, tok])
                        done = product(p_bank[:, 2 * a * P:2 * (a + 1) * P].rearrange("p (k m) -> p k m", k=2), terms)
                        done.then_inc(p_ready, 1)

                def transpose_p(pair):
                    if main:
                        pe.wait_ge(p_saved, PAIRS * i + pair + 1)
                        if not first or pair:
                            pe.wait_ge(s_ready, PAIRS * i + pair)
                        for a in range(2):
                            for k in range(2):
                                b = 2 * a + k
                                done = nc.tensor.transpose(pt_bank[:, b * P:(b + 1) * P], p_sb[:, pair, a, k, :], ident[:])
                        done.then_inc(pt_ready, 1)

                def norms_along_rows():
                    if finish:
                        pe.wait_ge(dvec_ready, i)
                        product(rk_bank[:], [(half_ones[:], d[:].rearrange("p k t m -> p (k t m)"))
                                             for d in (dvec_hi, dvec_lo)]).then_inc(rows_ready, 1)

                def transpose_k():
                    if finish:
                        pe.wait_ge(k_ready, i)
                        for t in range(T):
                            done = nc.tensor.transpose(rk_bank[:, t * P:(t + 1) * P], k_sb[:, t, :], ident[:])
                        done.then_inc(kt_ready, 1)

                def attend(t):
                    if finish:
                        if t == 0:
                            pe.wait_ge(kt_lo_done, i)
                            if tail:
                                pe.wait_ge(ring_lo, uses_to(g, ("u", 3), ends))
                        elif not tail or t == 3:
                            pe.wait_ge(o_added, T * (i - 1) + (1 if tail else t))
                        product(o_bank_of(t, tail)[:], three(kt_hi[:, t, :], kt_lo[:, t, :], u_hi[1 - parity][:, t, :],
                                                 u_lo[1 - parity][:, t, :])).then_inc(o_ready, 1)

                fill("y", LANG, 3)
                fill("y", LANG, 2)
                norms_along_rows()
                fill("y", GRAV, 3)
                fill("x", 0)
                fill("y", GRAV, 2)
                fill("x", 1)
                fill("y", LANG, 1)
                fill("x", 2)
                fill("y", GRAV, 1)
                fill("y", LANG, 0)
                fill("y", GRAV, 0)
                if tail:
                    fill("u", 3)
                fill("u", 0)
                transpose_k()
                fill("x", 3)
                inner_products(0)
                attend(0)
                inner_products(1)
                attend(1)
                if not last:
                    fill("u", 1)
                    attend(2)
                    transpose_p(0)
                    inner_products(2)
                    attend(3)
                    inner_products(3)
                    fill("u", 2)
                    transpose_p(1)
                    if main:
                        fill("u", 3)
                else:
                    transpose_p(0)
                    inner_products(2)
                    attend(2)
                    inner_products(3)
                    transpose_p(1)
                    attend(3)
                    fill("u", 1)
                    fill("u", 2)

            each_iteration(pe, body)


_INS = ["x", "adj", "L0_gnn_W_lang", "L0_gnn_W_grav", "L0_gnn_W_V", "L0_gnn_W_O", "L0_gnn_gate_logit",
        "L0_gnn_log_sigma"]
_OUTS = [((128, 64, 512), "float32")]


def kernel(**inputs):
    import numpy as _np
    import concourse.bacc as _bacc
    from concourse import mybir as _mybir
    from concourse.bass_utils import run_bass_kernel_spmd as _run

    nc = _bacc.Bacc("TRN2", target_bir_lowering=False, num_devices=1)
    arrays, args = {}, []
    for name in _INS:
        a = _np.ascontiguousarray(inputs[name])
        if a.ndim < 2:
            a = a.reshape(1, 1)
        arrays[f"in_{name}_dram"] = a
        args.append(nc.dram_tensor(f"in_{name}_dram", a.shape, _mybir.dt.from_np(a.dtype), kind="ExternalInput").ap())
    for i, (shape, dtype) in enumerate(_OUTS):
        dt = _mybir.dt.from_np(_np.dtype(dtype))
        args.append(nc.dram_tensor(f"out_{i}_dram", shape, dt, kind="ExternalOutput").ap())
    graph_attention_kernel(nc, *args)
    r = _run(nc, [arrays], core_ids=[0])
    got = tuple(r.results[0][f"out_{i}_dram"] for i in range(len(_OUTS)))
    return got[0]
```
